# Optimizing a Trainium2 kernel written in Bass

```python
import numpy as np
import jax
import jax.numpy as jnp

def _softmax(x, axis=-1):
    return jax.nn.softmax(x, axis=axis)

def _gelu(x):
    return jax.nn.gelu(x, approximate=True)

def _silu(x):
    return jax.nn.silu(x)

def _sigmoid(x):
    return jax.nn.sigmoid(x)

def _layernorm(x, axis=-1, eps=1e-05):
    m = jnp.mean(x, axis=axis, keepdims=True)
    v = jnp.var(x, axis=axis, keepdims=True)
    return (x - m) / jnp.sqrt(v + eps)

def _scatter_add(tgt, idx, src, axis=0):
    return tgt.at[idx].add(src)

def _segment_sum(src, seg, n):
    return jax.ops.segment_sum(src, seg, n)
kernel_name = 'mk_adj_resnorm_d2_adj_r2_c0cbb4'

def setup_inputs(seed: int=0):
    np.random.seed(seed)
    _w = jnp.asarray

    def _rec_inputs():
        import jax
        import jax.numpy as jnp
        _gk = jax.random.key(seed)
        x = -0.006082 + 1.001 * jax.random.normal(jax.random.fold_in(_gk, 1), (64, 128, 64), jnp.float32)
        _a = jax.random.bernoulli(jax.random.fold_in(_gk, 2), 0.125, (64, 128, 128))
        _a = jnp.logical_or(_a, jnp.swapaxes(_a, -1, -2))
        _a = jnp.logical_or(_a, jnp.eye(128, dtype=bool))
        _af = _a.astype(jnp.float32)
        _af = _af * jax.random.uniform(jax.random.fold_in(_gk, 3), (64, 128, 128), jnp.float32, 0.05, 4.42607)
        adj = _af
        return (x, adj)
    x, adj = _rec_inputs()

    def _L0_gnn_setup():
        import jax, jax.numpy as jnp
        import numpy as np
        key = jax.random.key(seed)
        ks = jax.random.split(key, 6)
        B, N, F, H, O = (2, 256, 64, 192, 64)
        x = jax.random.normal(ks[0], (B, N, F), dtype=jnp.float32)
        adj = jax.random.normal(ks[1], (B, N, N), dtype=jnp.float32)
        W1 = jax.random.normal(ks[2], (2 * F, H), dtype=jnp.float32) * (1.0 / np.sqrt(2 * F))
        b1 = jax.random.normal(ks[3], (H,), dtype=jnp.float32) * 0.02
        W2 = jax.random.normal(ks[4], (H, O), dtype=jnp.float32) * (1.0 / np.sqrt(H))
        b2 = jax.random.normal(ks[5], (O,), dtype=jnp.float32) * 0.02
        return {'x': x, 'adj': adj, 'W1': W1, 'b1': b1, 'W2': W2, 'b2': b2}
    _L0_gnn_all = _L0_gnn_setup()
    _L0_gnn_in = {k: v for k, v in _L0_gnn_all.items() if k in ('W1', 'b1', 'W2', 'b2')}
    del _L0_gnn_all

    def _L1_gnn_setup():
        import jax, jax.numpy as jnp
        import numpy as np
        B, L, C, OUT = (32, 512, 64, 64)
        BN_EPS = 1e-05
        key = jax.random.key(seed)
        kH, kA, kW = jax.random.split(key, 3)
        H = jax.random.normal(kH, (B, L, C), dtype=jnp.float32)
        A = jax.random.uniform(kA, (B, L, L), dtype=jnp.float32)
        gamma = jnp.ones((C,), jnp.float32)
        beta = jnp.zeros((C,), jnp.float32)
        W = jax.random.normal(kW, (C, OUT), dtype=jnp.float32) * 0.05
        b = jnp.zeros((OUT,), jnp.float32)
        return {'H': H, 'A': A, 'gamma': gamma, 'beta': beta, 'W': W, 'b': b}
    _L1_gnn_all = _L1_gnn_setup()
    _L1_gnn_in = {k: v for k, v in _L1_gnn_all.items() if k in ('gamma', 'beta', 'W', 'b')}
    del _L1_gnn_all
    return {'x': x, 'adj': adj, 'L0_gnn_W1': _L0_gnn_in['W1'], 'L0_gnn_b1': _L0_gnn_in['b1'], 'L0_gnn_W2': _L0_gnn_in['W2'], 'L0_gnn_b2': _L0_gnn_in['b2'], 'L1_gnn_gamma': _L1_gnn_in['gamma'], 'L1_gnn_beta': _L1_gnn_in['beta'], 'L1_gnn_W': _L1_gnn_in['W'], 'L1_gnn_b': _L1_gnn_in['b']}

def reference(x, adj, L0_gnn_W1, L0_gnn_b1, L0_gnn_W2, L0_gnn_b2, L1_gnn_gamma, L1_gnn_beta, L1_gnn_W, L1_gnn_b):
    import jax
    import jax.numpy as jnp

    def _L0_gnn_ref(x, adj, W1, b1, W2, b2):
        import jax, jax.numpy as jnp
        import numpy as np
        F = x.shape[-1]
        mask = (adj > 0.0).astype(x.dtype)
        W1a, W1b = (W1[:F], W1[F:])
        xj_proj = x @ W1a
        diff = x[:, :, None, :] - x[:, None, :, :]
        h = jax.nn.relu(xj_proj[:, :, None, :] + diff @ W1b + b1)
        hm = jnp.einsum('bjkh,bjk->bjh', h, mask)
        deg = jnp.sum(mask, axis=-1)
        return hm @ W2 + deg[..., None] * b2

    def _L1_gnn_ref(H, A, gamma, beta, W, b):
        import jax, jax.numpy as jnp
        import numpy as np
        B, L, C, OUT = (32, 512, 64, 64)
        BN_EPS = 1e-05
        batch, l, c = H.shape
        Hf = H.reshape(batch * l, c)
        mean = Hf.mean(axis=0)
        var = jnp.mean((Hf - mean) ** 2, axis=0)
        Hn = ((Hf - mean) * jax.lax.rsqrt(var + BN_EPS) * gamma + beta).reshape(batch, l, c)
        d = A.sum(axis=2)
        A_norm = jnp.sqrt(d)[:, :, None] * A * jax.lax.rsqrt(d)[:, None, :]
        A_hat = jnp.eye(l, dtype=A.dtype) - A_norm
        X = Hn @ W + b
        out = jnp.einsum('bij,bjo->bio', A_hat, X)
        return jax.nn.leaky_relu(out, negative_slope=0.01)
    x = _layernorm(x + _L0_gnn_ref(x, adj, L0_gnn_W1, L0_gnn_b1, L0_gnn_W2, L0_gnn_b2), axis=-1)
    x = _layernorm(x + _L1_gnn_ref(x, adj, L1_gnn_gamma, L1_gnn_beta, L1_gnn_W, L1_gnn_b), axis=-1)
    return x

_drawn_inputs = setup_inputs


def setup_inputs(seed=0):
    import zlib

    import numpy as np

    out = dict(_drawn_inputs(seed))
    spreads = {'L1_gnn_gamma': (1.0, 0.2), 'L1_gnn_beta': (0.0, 0.1), 'L1_gnn_b': (0.0, 0.1)}
    factors = {'L0_gnn_b1': 6.339, 'L0_gnn_b2': 8.0}
    for name, (base, spread) in spreads.items():
        noise = np.random.default_rng([zlib.crc32(name.encode()), seed]).standard_normal(out[name].shape)
        drawn = base * np.exp(spread * noise) if base else spread * noise
        out[name] = jnp.asarray(drawn.astype(out[name].dtype))
    for name, factor in factors.items():
        out[name] = (out[name] * factor).astype(out[name].dtype)
    return out
```

```python
import concourse.bass as bass
from concourse import mybir
from contextlib import ExitStack


def gnn_kernel(nc, x, adj, W1, b1, W2, b2, gamma, beta, W, bvec, out):
    f32, bf16 = mybir.dt.float32, mybir.dt.bfloat16
    ALU, ACT, AX = mybir.AluOpType, mybir.ActivationFunctionType, mybir.AxisListType

    NB, N, F = x.shape
    H = W1.shape[1]
    EPS = 1e-5
    HU = 4
    UNITS = H // HU
    SETS = 8
    C1, HQ = 3, 2
    HH = H // 2
    HALF_UNITS = UNITS // 2
    PARTS = 3
    PROWS, QROWS = PARTS, PARTS * HU
    QP0 = PROWS * SETS
    BANKS = 4
    LAG = 4
    RING = 4
    BIG = float(2 ** 60)
    PAIRS = NB // 2
    EU = UNITS // 2
    WLOADS, QSTORES = SETS, C1
    assert UNITS == SETS * C1 * HQ and N == 128 and 2 * F == 128

    ctx = ExitStack()
    with ctx:
        def sb(name, shape, dt=f32):
            return ctx.enter_context(nc.sbuf_tensor(name, shape, dt))

        def sem(name):
            return ctx.enter_context(nc.semaphore(name))

        GB = 8
        GROUPS = NB // GB

        wq = [sb(f"wq{i}", [128, C1, SETS, HQ, N]) for i in range(2)]
        mv = [sb(f"mv{i}", [128, HU, C1, HQ, N]) for i in range(2)]
        tparts = [sb(f"tparts{i}", [HH, PARTS, 2, HQ, N]) for i in range(2)]
        at_all = sb("at_all", [128, NB, N])
        x_all = sb("x_all", [128, NB, F])
        x1t_all = sb("x1t_all", [128, PAIRS, N])
        a_in = [sb(f"a_in{i}", [128, N]) for i in range(2)]
        x_in = sb("x_in", [128, 2, F])
        xt = sb("xt", [128, N])
        qn = [sb(f"qn{i}", [128, PARTS + 1, H]) for i in range(2)]
        pn = [sb(f"pn{i}", [128, H]) for i in range(2)]
        ind_a = [sb(f"ind_a{i}", [128, HU * N], bf16) for i in range(RING)]
        ind_v = [sb(f"ind_v{i}", [128, HU * N], bf16) for i in range(RING)]
        mask = [sb(f"mask{i}", [128, N], bf16) for i in range(2)]
        nmask = [sb(f"nmask{i}", [128, N], bf16) for i in range(2)]
        sums = [sb(f"sums{i}", [128, 2, PARTS + 1, HH]) for i in range(2)]
        hm = sb("hm", [128, 2, HH])
        hm_t = sb("hm_t", [HH, 2, N])
        d_all = sb("d_all", [128, NB])
        x1 = sb("x1", [128, 2, F])
        ln_stats = sb("ln_stats", [128, 6])
        ln_mv = sb("ln_mv", [128, 2])
        ln_var = sb("ln_var", [128, 1])
        ln_rstd = sb("ln_rstd", [128, 1])
        eps = sb("eps", [128, GB])
        half_up = sb("half_up", [128, NB])
        half_down = sb("half_down", [128, NB])
        ident = sb("ident", [128, 128])
        neg_big = sb("neg_big", [128, 128], bf16)
        pat_w = sb("pat_w", [128, SETS])
        pat_m = sb("pat_m", [128, HU])
        ones = sb("ones", [1, 128])
        w_raw = sb("w_raw", [128, 2, H])
        w_sign = sb("w_sign", [128, 2, H])
        w_diff = sb("w_diff", [128, 2, H])
        w_nat = [sb(f"w_nat{i}", [128, 2, H]) for i in range(2)]
        w_t = [sb(f"w_t{i}", [128, 2, HQ, HH]) for i in range(2)]
        b1_row = sb("b1_row", [1, H])
        b1_diff = sb("b1_diff", [1, H])
        b1_t = sb("b1_t", [1, HQ, HH])
        b2_row = sb("b2_row", [1, F])
        b1_all = sb("b1_all", [128, H])
        b1t_all = sb("b1t_all", [HH, HQ, N])
        b2_parts = sb("b2_parts", [128, PARTS, F])
        w2_sb = sb("w2_sb", [HH, 2, F])
        lw = sb("lw", [128, F])
        lb_row = sb("lb_row", [1, F])
        gb = sb("gb", [128, 2])
        havg = sb("havg", [128, 128])
        hdif = sb("hdif", [128, 128])
        bn_st = sb("bn_st", [128, 8, 6])
        bn_mv = sb("bn_mv", [128, 2])
        bn = sb("bn", [128, 8])
        w_bn = sb("w_bn", [128, 2, F])
        shift = sb("shift", [F, N])
        e_all = sb("e_all", [128, F])
        rs_all = sb("rs_all", [128, NB])
        sd_all = sb("sd_all", [128, NB])
        l1_tiles = wq[0][:, :, :, :, :].rearrange("p c s q k -> p (c s q k)").rearrange(
            "p (t b f) -> p t b f", b=GB, f=F)
        xe, ys, zz, zl, y2, yf = ([l1_tiles[:, 2 * t + i] for i in range(2)] for t in range(6))
        g_st = sb("g_st", [128, GB, 6])
        g_mv = sb("g_mv", [128, GB, 2])
        g_rstd = sb("g_rstd", [128, GB])

        d_bank = [ctx.enter_context(nc.psum_tensor(f"d_bank{i}", [128, 512], f32)) for i in range(BANKS)]
        s_bank = [ctx.enter_context(nc.psum_tensor(f"s_bank{i}", [128, 512], f32)) for i in range(2)]
        bx = ctx.enter_context(nc.psum_tensor("bx", [128, 512], f32))
        by = ctx.enter_context(nc.psum_tensor("by", [128, 512], f32))

        q_dram = [nc.dram_tensor(f"q_scratch{i}", (SETS, HU, PARTS, C1, HQ * N), f32, kind="Internal").ap()
                  for i in range(2)]
        p_dram = [nc.dram_tensor(f"p_scratch{i}", (PARTS, HH, HQ * N), f32, kind="Internal").ap()
                  for i in range(2)]

        w1_in, w2_in, b_in, l1_in, x_all_in = (sem(n) for n in ("w1_in", "w2_in", "b_in", "l1_in", "x_all_in"))
        a_loaded, x_loaded = [sem(f"a_loaded{i}") for i in range(2)], sem("x_loaded")
        pool_step, dve_step, act_setup = sem("pool_step"), sem("dve_step"), sem("act_setup")
        pats_ready, ident_ready, weights_ready = sem("pats_ready"), sem("ident_ready"), sem("weights_ready")
        bias_psum, bias_ready, qn_ones = sem("bias_psum"), sem("bias_ready"), sem("qn_ones")
        operands_init = sem("operands_init")
        xt_psum, xt_copied = sem("xt_psum"), sem("xt_copied")
        at_psum, at_copied = sem("at_psum"), sem("at_copied")
        t_psum, t_copied, tq_split, tp_split = (sem(n) for n in ("t_psum", "t_copied", "tq_split", "tp_split"))
        pq_psum, pq_copied, q_split = sem("pq_psum"), sem("pq_copied"), sem("q_split")
        q_stored, p_stored = sem("q_stored"), sem("p_stored")
        wq_loaded, mv_loaded = sem("wq_loaded"), sem("mv_loaded")
        d_done, masks_made = sem("d_done"), sem("masks_made")
        d_for_act, d_for_dve = sem("d_for_act"), sem("d_for_dve")
        act_ind, dve_ind, contracted = sem("act_ind"), sem("dve_ind"), sem("contracted")
        s_copied, hm_step, hm_ready = sem("s_copied"), sem("hm_step"), sem("hm_ready")
        hmt_psum, hmt_copied, l0_psum, l0_added = (sem(n) for n in ("hmt_psum", "hmt_copied", "l0_psum", "l0_added"))
        ln_step, x1_ready, x1_kept = sem("ln_step"), sem("x1_ready"), sem("x1_kept")
        x1t_psum, x1t_copied = sem("x1t_psum"), sem("x1t_copied")
        t_step, q_step, pow_consts = sem("t_step"), sem("q_step"), sem("pow_consts")
        var_ready, rstd_step, rstd_ready = sem("var_ready"), sem("rstd_step"), sem("rstd_ready")
        bn_var, bn_rstd, g_var, g_rstd_ready = sem("bn_var"), sem("bn_rstd"), sem("g_var"), sem("g_rstd_ready")
        bn_ready, bn_comb, wbn_ready, e_psum = sem("bn_ready"), sem("bn_comb"), sem("wbn_ready"), sem("e_psum")
        rs_ready, xw_psum, xe_ready, ys_ready = sem("rs_ready"), sem("xw_psum"), sem("xe_ready"), sem("ys_ready")
        ay_psum, zz_ready, zl_ready = sem("ay_psum"), sem("zz_ready"), sem("zl_ready")
        zd_ready, y2_ready, mv_ready, yc_ready = sem("zd_ready"), sem("y2_ready"), sem("mv_ready"), sem("yc_ready")
        yf_ready, out_stored = sem("yf_ready"), [sem(f"out_stored{i}") for i in range(2)]

        block = ctx.enter_context(nc.Block())

        def hi(ap):
            return ap.bitcast(bf16)

        def graphs(eng, program):
            program(0, 0, True, False)
            program(1, 1, False, False)
            with eng.Fori(1, PAIRS - 1) as pair:
                program(2 * pair, 0, False, False)
                program(2 * pair + 1, 1, False, False)
            program(NB - 2, 0, False, False, True)
            program(NB - 1, 1, False, True, True)

        @block.sync
        def _(sp):
            sp.dma_start(x_in[:, :, :], x[0:2].rearrange("b j f -> j b f")).then_inc(x_loaded, 16)
            w1_v = W1.rearrange("(t f) h -> f t h", t=2)
            sp.dma_start(w_raw[0:F], w1_v).then_inc(w1_in, 16)
            sp.dma_start(w_raw[F:128], w1_v).then_inc(w1_in, 16)
            sp.dma_start(b1_row[:, :], b1.rearrange("(a h) -> a h", a=1)).then_inc(b_in, 16)
            sp.dma_start(b2_row[:, :], b2.rearrange("(a h) -> a h", a=1)).then_inc(b_in, 16)
            sp.dma_start(lb_row[:, :], bvec.rearrange("(a h) -> a h", a=1)).then_inc(b_in, 16)
            for i in range(2):
                sp.dma_start(a_in[i][:, :], adj[i]).then_inc(a_loaded[i], 16)
            sp.dma_start(w2_sb[:, :, :], W2.rearrange("(t h) o -> h t o", t=2)).then_inc(w2_in, 16)
            for i in range(2):
                rows = slice(F * i, F * i + F)
                sp.dma_start(lw[rows], W).then_inc(l1_in, 16)
                sp.dma_start(gb[rows, 0:1], gamma.rearrange("(c a) -> c a", a=1)).then_inc(l1_in, 16)
                sp.dma_start(gb[rows, 1:2], beta.rearrange("(c a) -> c a", a=1)).then_inc(l1_in, 16)
            sp.dma_start(x_all[:, :, :], x.rearrange("b j f -> j b f")).then_inc(x_all_in, 16)

            def value(v):
                if isinstance(v, int):
                    return v
                reg = sp.alloc_register()
                sp.reg_mov(reg, v)
                return sp.snap(reg, donate=True)

            def counts(n):
                return {"parts": value(n + 1), "wq_before": value(16 * WLOADS * (n - 1)),
                        "mv_before": value(16 * (n - 1)), "d_before": value(EU * (n - 1)),
                        "q_stored": value(16 * QSTORES * (n + 1)), "p_stored": value(16 * (n + 1))}

            def operands(cnt, par, first_use):
                sp.wait_ge(tq_split, cnt["parts"])
                if not first_use:
                    sp.wait_ge(wq_loaded, cnt["wq_before"])
                    sp.wait_ge(mv_loaded, cnt["mv_before"])
                for c1 in range(C1):
                    sp.dma_start(q_dram[par][:, :, :, c1].rearrange("s h i k -> (s h) i k"),
                                 tparts[par][c1:HH:C1, :, 1].rearrange("p i q k -> p i (q k)")).then_inc(q_stored, 16)
                sp.wait_ge(tp_split, cnt["parts"])
                sp.dma_start(p_dram[par].rearrange("i t k -> t i k"),
                             tparts[par][:, :, 0].rearrange("p i q k -> p i (q k)")).then_inc(p_stored, 16)
                if first_use:
                    sp.wait_ge(operands_init, 4)
                else:
                    sp.wait_ge(d_for_dve, cnt["d_before"])
                sp.wait_ge(q_stored, cnt["q_stored"])
                for s in range(SETS):
                    sp.dma_start(wq[par][QP0 + s:QP0 + SETS * QROWS:SETS, :, s].rearrange("r c q k -> r c (q k)"),
                                 q_dram[par][s].rearrange("h i c k -> (h i) c k")).then_inc(wq_loaded, 16)
                sp.wait_ge(p_stored, cnt["p_stored"])
                sp.dma_start(mv[par][0:QP0].rearrange("p h c q k -> p (h c q k)"),
                             p_dram[par].rearrange("i (s m) k -> (i s) (m k)", s=SETS)).then_inc(mv_loaded, 16)

            operands(counts(0), 0, True)

            def graph(b, par, first, last, last_pair=False):
                ahead, done, pairs_done = value(b + 2), value(b + 1), value(b // 2 + 1)
                cnt = counts(b + 1)
                if not last_pair:
                    sp.wait_ge(at_psum, done)
                    sp.wait_ge(d_done, done)
                    sp.dma_start(a_in[par][:, :], adj[bass.ds(ahead, 1)].rearrange("a j k -> (a j) k"))\
                        .then_inc(a_loaded[par], 16)
                if not last:
                    operands(cnt, 1 - par, first)
                if par == 0 and not last_pair:
                    sp.wait_ge(xt_psum, pairs_done)
                    sp.dma_start(x_in[:, :, :], x[bass.ds(ahead, 2)].rearrange("b j f -> j b f"))\
                        .then_inc(x_loaded, 16)

            graphs(sp, graph)

            for g in range(GROUPS):
                sp.wait_ge(yf_ready, g + 1)
                sp.dma_start(out[GB * g:GB * g + GB].rearrange("b j o -> j b o"), yf[g % 2][:, :, :])\
                    .then_inc(out_stored[g % 2], 16)
            for i in range(2):
                sp.wait_ge(out_stored[i], 16 * (GROUPS // 2))

        @block.gpsimd
        def _(pool):
            steps = [0]

            def link(ins):
                steps[0] += 1
                ins.then_inc(pool_step, 1)
                pool.wait_ge(pool_step, steps[0])

            nc.gpsimd.memset(eps[:, :], EPS).then_inc(pow_consts, 1)
            nc.gpsimd.memset(half_up[:, :], 0.5).then_inc(pow_consts, 1)
            nc.gpsimd.memset(half_down[:, :], -0.5).then_inc(pow_consts, 1)
            link(nc.gpsimd.memset(pat_w[:, :], 0.0))
            for i in range(PROWS):
                link(nc.gpsimd.affine_select(out=pat_w[:, :], in_=pat_w[:, :], compare_op=ALU.not_equal, fill=1.0,
                                             base=-SETS * i, pattern=[[-1, SETS]], channel_multiplier=1))
            rows = SETS * PARTS
            link(nc.gpsimd.memset(pat_m[:, :], 1.0))
            link(nc.gpsimd.affine_select(out=pat_m[:, :], in_=pat_m[:, :], compare_op=ALU.is_ge, fill=0.0,
                                         base=-QP0, pattern=[[-rows, HU]], channel_multiplier=1))
            nc.gpsimd.affine_select(out=pat_m[:, :], in_=pat_m[:, :], compare_op=ALU.is_ge, fill=0.0,
                                    base=QP0 + rows - 1, pattern=[[rows, HU]], channel_multiplier=-1)\
                .then_inc(pats_ready, 1)
            link(nc.gpsimd.memset(ident[:, :], 0.0))
            nc.gpsimd.affine_select(out=ident[:, :], in_=ident[:, :], compare_op=ALU.not_equal, fill=1.0,
                                    base=0, pattern=[[-1, 128]], channel_multiplier=1).then_inc(ident_ready, 1)
            for i in range(2):
                nc.gpsimd.memset(qn[i][:, PARTS], 1.0).then_inc(qn_ones, 1)

            def split_t(n, par):
                pool.wait_ge(t_copied, n + 1)
                for t in (1, 0):
                    for i in range(1, PARTS):
                        part = tparts[par][:, i, t].rearrange("p q k -> p (q k)")
                        before = tparts[par][:, i - 1, t].rearrange("p q k -> p (q k)")
                        if i == 2:
                            pool.wait_ge(t_step, 2 * n + (1 if t else 2))
                        nc.gpsimd.tensor_tensor(part, before, hi(before)[:, 1::2], ALU.subtract)\
                            .then_inc(t_step if i == 1 else tq_split if t else tp_split, 1)

            def split_q(n, par):
                pool.wait_ge(pq_copied, n + 1)
                nc.gpsimd.tensor_tensor(pn[par][:, :], pn[par][:, :], b1_all[:, :], ALU.add).then_inc(q_step, 1)
                for i in range(1, PARTS):
                    t = qn[par]
                    if i == 2:
                        pool.wait_ge(q_step, 2 * n + 2)
                    nc.gpsimd.tensor_tensor(t[:, i], t[:, i - 1], hi(t[:, i - 1])[:, 1::2], ALU.subtract)\
                        .then_inc(q_step if i == 1 else q_split, 1)

            def finish_hm(o, par, first):
                pool.wait_ge(s_copied, 2 * o + 2)
                if not first:
                    pool.wait_ge(hmt_psum, o)
                nc.gpsimd.tensor_tensor(hm[:, :, :], pn[par][:, :].rearrange("p (t h) -> p t h", t=2),
                                        sums[par][:, :, PARTS], ALU.mult).then_inc(hm_step, 1)
                for i in range(PARTS):
                    pool.wait_ge(hm_step, PARTS * o + i + 1)
                    nc.gpsimd.tensor_tensor(hm[:, :, :], hm[:, :, :], sums[par][:, :, i], ALU.subtract)\
                        .then_inc(hm_ready if i == PARTS - 1 else hm_step, 1)

            def rstd(o):
                pool.wait_ge(var_ready, o + 1)
                nc.gpsimd.tensor_tensor(ln_var[:, :], ln_mv[:, 1:2], eps[:, 0:1], ALU.add).then_inc(rstd_step, 1)
                pool.wait_ge(rstd_step, o + 1)
                nc.gpsimd.tensor_tensor(ln_rstd[:, :], ln_var[:, :], half_down[:, 0:1], ALU.pow)\
                    .then_inc(rstd_ready, 1)

            pool.wait_ge(pow_consts, 3)
            pool.wait_ge(bias_ready, 1)
            split_t(0, 0)
            split_q(0, 0)

            def graph(b, par, first, last, last_pair=False):
                if not last:
                    split_t(b + 1, 1 - par)
                if not first:
                    finish_hm(b - 1, 1 - par, isinstance(b, int) and b == 1)
                    rstd(b - 1)
                if not last:
                    split_q(b + 1, 1 - par)
                if par == 0 and not first:
                    keep_x1(b)

            def keep_x1(b):
                pool.wait_ge(x1_ready, b)
                pool_copy = nc.gpsimd.tensor_copy(x_all[:, bass.ds(b - 2, 2)], x1[:, :, :])
                pool_copy.then_inc(x1_kept, 1)

            graphs(pool, graph)
            finish_hm(NB - 1, 1, False)
            rstd(NB - 1)
            keep_x1(NB)

            pool.wait_ge(d_done, NB)
            nc.gpsimd.tensor_tensor(sd_all[:, :], d_all[:, :], half_up[:, :], ALU.pow).then_inc(rs_ready, 1)
            nc.gpsimd.tensor_tensor(rs_all[:, :], d_all[:, :], half_down[:, :], ALU.pow).then_inc(rs_ready, 1)
            pool.wait_ge(bn_var, 1)
            nc.gpsimd.tensor_tensor(bn[:, 4:5], bn[:, 3:4], half_down[:, 0:1], ALU.pow).then_inc(bn_rstd, 1)
            for g in range(GROUPS):
                i = g % 2
                b0 = GB * g
                pool.wait_ge(xe_ready, g + 1)
                if g == 0:
                    pool.wait_ge(rs_ready, 2)
                if g >= 2:
                    pool.wait_ge(ay_psum, g - 1)
                nc.gpsimd.tensor_tensor(ys[i][:, :, :], xe[i][:, :, :],
                                        rs_all[:, b0:b0 + GB].unsqueeze(2).broadcast_to([128, GB, F]), ALU.mult)\
                    .then_inc(ys_ready, 1)
                pool.wait_ge(zz_ready, g + 1)
                nc.gpsimd.tensor_tensor(zz[i][:, :, :], xe[i][:, :, :], zz[i][:, :, :], ALU.subtract)\
                    .then_inc(zd_ready, 1)
                pool.wait_ge(zl_ready, g + 1)
                if g == 0:
                    pool.wait_ge(x1_kept, PAIRS)
                if g >= 2:
                    pool.wait_ge(yc_ready, g - 1)
                nc.gpsimd.tensor_tensor(y2[i][:, :, :], zl[i][:, :, :], x_all[:, b0:b0 + GB], ALU.add)\
                    .then_inc(y2_ready, 1)
                pool.wait_ge(mv_ready, g + 1)
                nc.gpsimd.tensor_tensor(y2[i][:, :, :], y2[i][:, :, :],
                                        g_mv[:, :, 0:1].broadcast_to([128, GB, F]), ALU.subtract)\
                    .then_inc(yc_ready, 1)
                pool.wait_ge(g_var, g + 1)
                nc.gpsimd.tensor_tensor(g_rstd[:, :], g_rstd[:, :], half_down[:, 0:GB], ALU.pow)\
                    .then_inc(g_rstd_ready, 1)

        @block.scalar
        def _(act):
            act.wait_ge(pats_ready, 1)
            nc.scalar.activation(mv[0][:, :, :, :, :].rearrange("p h c q k -> p h (c q k)"),
                                 pat_m[:, :].unsqueeze(2).broadcast_to([128, HU, C1 * HQ * N]), ACT.Copy)\
                .then_inc(operands_init, 1)
            nc.scalar.activation(mv[1][:, :, :, :, :].rearrange("p h c q k -> p h (c q k)"),
                                 pat_m[:, :].unsqueeze(2).broadcast_to([128, HU, C1 * HQ * N]), ACT.Copy)\
                .then_inc(operands_init, 1)

            def copy_xt(pair):
                act.wait_ge(xt_psum, pair + 1)
                nc.scalar.activation(xt[:, :], by[:, 0:N], ACT.Copy).then_inc(xt_copied, 1)

            def copy_at(n):
                act.wait_ge(at_psum, n + 1)
                nc.scalar.activation(at_all[:, bass.ds(n, 1)].rearrange("p a k -> p (a k)"), by[:, 0:N], ACT.Copy)\
                    .then_inc(at_copied, 1)

            def copy_pq(n, par, first_use):
                act.wait_ge(pq_psum, n + 1)
                if not first_use:
                    act.wait_ge(contracted, UNITS * (n - 1))
                    act.wait_ge(hm_ready, n - 1)
                nc.scalar.activation(pn[par][:, :], bx[:, 0:H], ACT.Copy)
                nc.scalar.activation(qn[par][:, 0], bx[:, H:2 * H], ACT.Copy).then_inc(pq_copied, 1)

            def copy_sums(b, par, half, first_use):
                act.wait_ge(contracted, UNITS * b + HALF_UNITS * (half + 1))
                if not first_use and half == 0:
                    act.wait_ge(hm_ready, b - 1)
                nc.scalar.activation(sums[par][:, half].rearrange("p i h -> p (i h)"),
                                     s_bank[half][:, 0:(PARTS + 1) * HH], ACT.Copy).then_inc(s_copied, 1)

            def copy_hmt(o, first_use):
                act.wait_ge(hmt_psum, o + 1)
                if not first_use:
                    act.wait_ge(l0_psum, o)
                nc.scalar.activation(hm_t[:, :, :].rearrange("p t k -> p (t k)"), by[0:HH, 0:2 * N], ACT.Copy)\
                    .then_inc(hmt_copied, 1)

            def copy_x1t(pair):
                act.wait_ge(x1t_psum, pair + 1)
                nc.scalar.activation(x1t_all[:, bass.ds(pair, 1)].rearrange("p a k -> p (a k)"), by[:, 0:N], ACT.Copy)\
                    .then_inc(x1t_copied, 1)

            copy_xt(0)
            copy_at(0)
            copy_pq(0, 0, True)
            nc.scalar.preload_act_table(ACT.Sigmoid)

            def graph(b, par, first, last, last_pair=False):
                for v in range(EU):
                    act.wait_ge(d_for_act, EU * b + v + 1)
                    if not (first and v < RING):
                        act.wait_ge(contracted, UNITS * b + 2 * (v - RING) + 1)
                    nc.scalar.activation(ind_a[v % RING][:, :], d_bank[2 * v % BANKS][:, :], ACT.Sigmoid, scale=BIG)\
                        .then_inc(act_ind, 1)
                    if v == 2 and not first:
                        copy_sums(b - 1, 1 - par, 1, True)
                    if v == 4 and not last:
                        copy_at(b + 1)
                    if v == 11 and not first:
                        copy_hmt(b - 1, isinstance(b, int) and b == 1)
                    if v == 14:
                        copy_sums(b, par, 0, isinstance(b, int) and b < 2)
                    if v == 16 and not last:
                        copy_pq(b + 1, 1 - par, first)
                    if v == 18 and par == 0 and not last_pair:
                        copy_xt(b // 2 + 1)
                    if v == 22 and par == 0 and not first:
                        copy_x1t(b // 2 - 1)

            graphs(act, graph)
            copy_sums(NB - 1, 1, 1, True)
            copy_hmt(NB - 1, False)
            copy_x1t(PAIRS - 1)

        @block.vector
        def _(dve):
            steps = [0]

            def link(ins):
                steps[0] += 1
                ins.then_inc(dve_step, 1)
                dve.wait_ge(dve_step, steps[0])

            link(nc.vector.memset(ones[:, :], 1.0))
            for i in range(2):
                link(nc.vector.memset(w_nat[i][:, :, :], 0.0))
                link(nc.vector.memset(w_t[i][:, :, :, :], 0.0))
            link(nc.vector.memset(w_bn[:, :, :], 0.0))
            dve.wait_ge(w1_in, 32)
            link(nc.vector.tensor_tensor(w_sign[:, 0], w_raw[:, 0], w_raw[:, 1], ALU.add))
            link(nc.vector.tensor_scalar(w_sign[:, 1], w_raw[:, 1], -1.0, None, ALU.mult))
            dve.wait_ge(b_in, 48)
            link(nc.vector.tensor_copy(w_diff[:, :, :], w_sign[:, :, :]))
            link(nc.vector.tensor_copy(b1_diff[:, :], b1_row[:, :]))

            def even_units(ap, a, b):
                return ap.rearrange("p (v k h) -> p v k h", k=2, h=HU)[:, a:b, 0]

            for dst, src in ((w_diff[:, 0], w_sign[:, 0]), (w_diff[:, 1], w_sign[:, 1]),
                             (b1_diff[:, :], b1_row[:, :])):
                link(nc.vector.tensor_tensor(even_units(dst, BANKS // 2, EU), even_units(src, BANKS // 2, EU),
                                             even_units(src, 0, EU - BANKS // 2), ALU.subtract))

            def reorder(dst, src):
                for q in range(HQ):
                    ins = nc.vector.tensor_copy(
                        dst[:, q].rearrange("p (m c) -> p c m", c=C1),
                        src.rearrange("p (c q m) -> p c q m", c=C1, q=HQ)[:, :, q])
                return ins

            for i in range(2):
                rows = slice(F * i, F * i + F)
                link(nc.vector.tensor_copy(w_nat[i][rows, 0], w_sign[rows, 0]))
                link(nc.vector.tensor_copy(w_nat[i][rows, 1], w_raw[rows, 1]))
                for t in range(2):
                    link(reorder(w_t[i][rows, t], w_diff[rows, t]))
            reorder(b1_t[:, :, :], b1_diff[:, :]).then_inc(weights_ready, 1)
            dve.wait_ge(ident_ready, 1)
            nc.vector.tensor_scalar(neg_big[:, :], ident[:, :], -BIG, None, ALU.mult).then_inc(weights_ready, 1)
            dve.wait_ge(bias_psum, 1)
            link(nc.vector.tensor_copy(b1_all[:, :], by[:, 0:H]))
            link(nc.vector.tensor_copy(b2_parts[:, 0], by[:, H:H + F]))
            for i in range(1, PARTS):
                link(nc.vector.tensor_tensor(b2_parts[:, i], b2_parts[:, i - 1], hi(b2_parts[:, i - 1])[:, 1::2],
                                             ALU.subtract))
            nc.vector.tensor_copy(b1t_all[:, :, :].rearrange("p q k -> p (q k)"), bx[0:HH, 0:HQ * N])\
                .then_inc(bias_ready, 1)

            def copy_t(n, par, first_use):
                dve.wait_ge(t_psum, n + 1)
                if not first_use:
                    dve.wait_ge(q_stored, 16 * QSTORES * (n - 1))
                    dve.wait_ge(p_stored, 16 * (n - 1))
                nc.vector.tensor_tensor(tparts[par][:, 0, 0].rearrange("p q k -> p (q k)"), bx[0:HH, 0:HQ * N],
                                        b1t_all[:, :, :].rearrange("p q k -> p (q k)"), ALU.add)
                nc.vector.tensor_copy(tparts[par][:, 0, 1].rearrange("p q k -> p (q k)"), bx[0:HH, HQ * N:2 * HQ * N])\
                    .then_inc(t_copied, 1)

            def degree(n, par):
                dve.wait_ge(a_loaded[par], 16 * (n // 2 + 1))
                nc.vector.tensor_reduce(d_all[:, bass.ds(n, 1)], a_in[par][:, :], AX.X, ALU.add).then_inc(d_done, 1)

            def make_masks(n, par):
                dve.wait_ge(at_copied, n + 1)
                at = at_all[:, bass.ds(n, 1)].rearrange("p a k -> p (a k)")
                nc.vector.tensor_scalar(mask[par][:, :], at, 0.0, None, ALU.is_gt)
                nc.vector.tensor_scalar(nmask[par][:, :], at, 0.0, None, ALU.is_le).then_inc(masks_made, 1)

            def norm_step(o, par, k):
                xo = x_all[:, bass.ds(o, 1)].rearrange("p a f -> p (a f)")
                if k == 0:
                    dve.wait_ge(l0_psum, o + 1)
                    if par == 0 and not (isinstance(o, int) and o == 0):
                        dve.wait_ge(x1_kept, o // 2)
                        dve.wait_ge(x1t_psum, o // 2)
                    nc.vector.tensor_tensor(x1[:, par], xo, bx[:, 0:F], ALU.add).then_inc(l0_added, 1)
                elif k == 1:
                    dve.wait_ge(l0_added, o + 1)
                    nc.vector.bn_stats(ln_stats[:, :], x1[:, par]).then_inc(ln_step, 1)
                elif k == 2:
                    nc.vector.bn_aggr(ln_mv[:, :], ln_stats[:, :]).then_inc(var_ready, 1)
                elif k == 3:
                    dve.wait_ge(rstd_ready, o + 1)
                    nc.vector.tensor_scalar(x1[:, par], x1[:, par], ln_mv[:, 0:1], ln_rstd[:, 0:1],
                                            ALU.subtract, ALU.mult).then_inc(x1_ready, 1)

            for i in range(2):
                dve.wait_ge(pats_ready, 1)
                nc.vector.tensor_copy(wq[i][:, :, :, :, :].rearrange("p c s q k -> p c s (q k)"),
                                      pat_w[:, :].unsqueeze(1).unsqueeze(3).broadcast_to([128, C1, SETS, HQ * N]))\
                    .then_inc(operands_init, 1)
                if i == 0:
                    copy_t(0, 0, True)
                    degree(0, 0)
                    make_masks(0, 0)
            link(nc.vector.memset(havg[:, :], 0.0))
            link(nc.vector.memset(hdif[:, :], 0.0))
            for i in range(2):
                for j in range(2):
                    r, c = slice(F * i, F * i + F), slice(F * j, F * j + F)
                    src = ident[r, r]
                    link(nc.vector.tensor_scalar(havg[r, c], src, 0.5, None, ALU.mult))
                    link(nc.vector.tensor_scalar(hdif[r, c], src, -0.5 if i else 0.5, None, ALU.mult))
            dve.wait_ge(x_all_in, 16)

            def graph(b, par, first, last, last_pair=False):
                for w in range(EU):
                    if w == 15 and not first:
                        dve.wait_ge(ln_step, b)
                    dve.wait_ge(d_for_dve, EU * b + w + 1)
                    if not (first and w < RING):
                        dve.wait_ge(contracted, UNITS * b + 2 * (w - RING) + 2)
                    nc.vector.scalar_tensor_tensor(
                        out=ind_v[w % RING][:, :].rearrange("p (h k) -> p h k", k=N),
                        in0=d_bank[(2 * w + 1) % BANKS][:, :].rearrange("p (h k) -> p h k", k=N), scalar=0.0,
                        in1=mask[par][:, :].unsqueeze(1).broadcast_to([128, HU, N]),
                        op0=ALU.is_gt, op1=ALU.mult).then_inc(dve_ind, 1)
                    if w == 0 and not last:
                        copy_t(b + 1, 1 - par, first)
                    if w == 4 and not last:
                        degree(b + 1, 1 - par)
                    if w in (13, 14, 15, 19) and not first:
                        norm_step(b - 1, 1 - par, min(w - 13, 3))
                    if w == 21 and not last:
                        make_masks(b + 1, 1 - par)

            graphs(dve, graph)
            for k in range(4):
                if k == 2:
                    dve.wait_ge(ln_step, NB)
                norm_step(NB - 1, 1, k)

            dve.wait_ge(x1t_copied, PAIRS)
            x1t_flat = x1t_all[:, :, :].rearrange("p a k -> p (a k)")
            for i in range(8):
                w = PAIRS * N // 8
                link(nc.vector.bn_stats(bn_st[:, i], x1t_flat[:, w * i:w * i + w]))
            nc.vector.bn_aggr(bn_mv[:, :], bn_st[:, :, :].rearrange("p a b -> p (a b)")).then_inc(bn_ready, 1)
            dve.wait_ge(bn_comb, 1)
            link(nc.vector.tensor_copy(bn[:, 0:3], bx[:, 0:3]))
            link(nc.vector.tensor_tensor(bn[:, 3:4], bn[:, 2:3], bn[:, 2:3], ALU.mult))
            nc.vector.tensor_scalar(bn[:, 3:4], bn[:, 3:4], bn[:, 1:2], EPS, ALU.add, ALU.add).then_inc(bn_var, 1)
            dve.wait_ge(bn_rstd, 1)
            dve.wait_ge(l1_in, 96)
            link(nc.vector.tensor_tensor(bn[:, 5:6], bn[:, 4:5], gb[:, 0:1], ALU.mult))
            link(nc.vector.tensor_tensor(bn[:, 6:7], bn[:, 0:1], bn[:, 5:6], ALU.mult))
            link(nc.vector.tensor_tensor(bn[:, 7:8], gb[:, 1:2], bn[:, 6:7], ALU.subtract))
            for i in range(2):
                r = slice(F * i, F * i + F)
                link(nc.vector.tensor_scalar(w_bn[r, i], lw[r], bn[r, 5:6], None, ALU.mult))
            nc.vector.tensor_copy(shift[:, :], bn[0:F, 7:8].broadcast_to([F, N])).then_inc(wbn_ready, 1)
            dve.wait_ge(e_psum, 1)
            link(nc.vector.tensor_copy(e_all[:, :], by[:, 0:F]))
            for g in range(GROUPS):
                i = g % 2
                b0 = GB * g
                dve.wait_ge(xw_psum, g + 1)
                if g >= 2:
                    dve.wait_ge(zd_ready, g - 1)
                nc.vector.tensor_tensor(xe[i][:, :, :], d_bank[i][:, :].rearrange("p (b f) -> p b f", f=F),
                                        e_all[:, :].unsqueeze(1).broadcast_to([128, GB, F]), ALU.add)\
                    .then_inc(xe_ready, 1)
                dve.wait_ge(ay_psum, g + 1)
                if g >= 2:
                    dve.wait_ge(zl_ready, g - 1)
                nc.vector.tensor_tensor(zz[i][:, :, :], d_bank[2 + i][:, :].rearrange("p (b f) -> p b f", f=F),
                                        sd_all[:, b0:b0 + GB].unsqueeze(2).broadcast_to([128, GB, F]), ALU.mult)\
                    .then_inc(zz_ready, 1)
                dve.wait_ge(zd_ready, g + 1)
                if g >= 2:
                    dve.wait_ge(y2_ready, g - 1)
                nc.vector.scalar_tensor_tensor(out=zl[i][:, :, :], in0=zz[i][:, :, :], scalar=0.01,
                                               in1=zz[i][:, :, :], op0=ALU.mult, op1=ALU.max).then_inc(zl_ready, 1)
                dve.wait_ge(y2_ready, g + 1)
                if g >= 1:
                    dve.wait_ge(yc_ready, g)
                for k in range(GB):
                    ins = nc.vector.bn_stats(g_st[:, k], y2[i][:, k])
                link(ins)
                for k in range(GB):
                    ins = nc.vector.bn_aggr(g_mv[:, k], g_st[:, k])
                ins.then_inc(mv_ready, 1)
                dve.wait_ge(mv_ready, g + 1)
                nc.vector.tensor_scalar(g_rstd[:, :], g_mv[:, :, 1], EPS, None, ALU.add).then_inc(g_var, 1)
                dve.wait_ge(g_rstd_ready, g + 1)
                dve.wait_ge(yc_ready, g + 1)
                if g >= 2:
                    dve.wait_ge(out_stored[i], 16 * (g // 2))
                nc.vector.tensor_tensor(yf[i][:, :, :], y2[i][:, :, :],
                                        g_rstd[:, :].unsqueeze(2).broadcast_to([128, GB, F]), ALU.mult)\
                    .then_inc(yf_ready, 1)

        @block.tensor
        def _(pe):
            def transpose_xt(pair):
                pe.wait_ge(x_loaded, 16 * (pair + 1))
                nc.tensor.transpose(by[:, 0:N], x_in[:, :, :].rearrange("p b f -> p (b f)"), ident[:, :])\
                    .then_inc(xt_psum, 1)

            def transpose_at(n, par):
                pe.wait_ge(a_loaded[par], 16 * (n // 2 + 1))
                nc.tensor.transpose(by[:, 0:N], a_in[par][:, :], ident[:, :]).then_inc(at_psum, 1)

            def project_t(n, par):
                for t in range(2):
                    for q in range(HQ):
                        k = (HQ * t + q) * N
                        ins = nc.tensor.matmul(bx[0:HH, k:k + N], w_t[par][:, t, q], xt[:, :], start=True, stop=True)
                ins.then_inc(t_psum, 1)

            def project_pq(n, par):
                nc.tensor.matmul(bx[:, 0:2 * H], xt[:, :], w_nat[par][:, :, :].rearrange("p t h -> p (t h)"),
                                 start=True, stop=True).then_inc(pq_psum, 1)

            def transpose_hm(o):
                pe.wait_ge(hm_ready, o + 1)
                for t in range(2):
                    ins = nc.tensor.transpose(by[0:HH, N * t:N * t + N], hm[:, t], ident[:, :])
                ins.then_inc(hmt_psum, 1)

            def layer0(o, par):
                pe.wait_ge(hmt_copied, o + 1)
                for t in range(2):
                    nc.tensor.matmul(bx[:, 0:F], hm_t[:, t], w2_sb[:, t], start=(t == 0), stop=False)
                for i in range(PARTS):
                    ins = nc.tensor.matmul(bx[:, 0:F], mask[par][:, :], hi(b2_parts[:, i])[:, 1::2],
                                           start=False, stop=(i == PARTS - 1))
                ins.then_inc(l0_psum, 1)

            def transpose_x1(pair):
                pe.wait_ge(x1_ready, 2 * pair + 2)
                nc.tensor.transpose(by[:, 0:N], x1[:, :, :].rearrange("p b f -> p (b f)"), ident[:, :])\
                    .then_inc(x1t_psum, 1)

            def contract(u, par):
                ring = ind_v if u % 2 else ind_a
                half, col = divmod(HU * u, HH)
                sums_out = s_bank[half][:, 0:(PARTS + 1) * HH].rearrange("p (i h) -> p i h", i=PARTS + 1)
                qv = hi(qn[par][:, :, :].rearrange("p i h -> p (i h)")).rearrange(
                    "p (i h e) -> p i h e", i=PARTS + 1, e=2)
                for h in range(HU):
                    ins = nc.tensor.matmul(sums_out[:, :, col + h],
                                           ring[(u // 2) % RING][:, N * h:N * h + N],
                                           qv[:, :, HU * u + h, 1], start=True, stop=True)
                ins.then_inc(contracted, 1)

            def difference(u, par):
                c, s = divmod(u, SETS)
                c1, q = divmod(c, HQ)
                bank = d_bank[u % BANKS]
                if u in (0, 2):
                    nc.tensor.matmul(bank[:, :].rearrange("p (h k) -> p h k", k=N), neg_big[:, :],
                                     nmask[par][:, :].unsqueeze(1).broadcast_to([128, HU, N]),
                                     start=True, stop=True, skip_group_check=True)
                wv = hi(wq[par][:, c1, s, q])[:, 1::2]
                m = hi(mv[par][:, :, :, :, :].rearrange("p h c q k -> p (h c q k)")).rearrange(
                    "p (h c q k e) -> p h c q k e", h=HU, c=C1, q=HQ, e=2)[:, :, c1, q, :, 1]
                nc.tensor.matmul(bank[:, :].rearrange("p (h k) -> p h k", k=N), wv, m, start=bool(u % 2), stop=True,
                                 skip_group_check=True)\
                    .then_inc(d_for_dve if u % 2 else d_for_act, 1)

            pe.wait_ge(weights_ready, 2)
            nc.tensor.matmul(by[:, 0:H], ones[:, :], b1_row[:, :], start=True, stop=True)
            nc.tensor.matmul(by[:, H:H + F], ones[:, :], b2_row[:, :], start=True, stop=True)
            for q in range(HQ):
                ins = nc.tensor.matmul(bx[0:HH, N * q:N * q + N], b1_t[:, q], ones[:, :], start=True, stop=True)
            ins.then_inc(bias_psum, 1)
            pe.wait_ge(bias_ready, 1)
            transpose_xt(0)
            pe.wait_ge(xt_copied, 1)
            project_t(0, 0)
            transpose_at(0, 0)
            pe.wait_ge(t_copied, 1)
            project_pq(0, 0)
            pe.wait_ge(qn_ones, 2)
            pe.wait_ge(w2_in, 16)

            def graph(b, par, first, last, last_pair=False):
                for u in range(UNITS):
                    if u == 0 and not last:
                        pe.wait_ge(pq_copied, b + 1)
                        if par == 1:
                            pe.wait_ge(xt_copied, b // 2 + 2)
                        project_t(b + 1, 1 - par)
                    if u == 6 and not last:
                        if par == 1:
                            pe.wait_ge(xt_copied, b // 2 + 2)
                            if not (isinstance(b, int) and b == 1):
                                pe.wait_ge(x1t_copied, b // 2)
                        elif first:
                            pe.wait_ge(at_copied, 1)
                        else:
                            pe.wait_ge(hmt_copied, b - 1)
                        transpose_at(b + 1, 1 - par)
                    if u == 20 and not first:
                        if last:
                            pe.wait_ge(x1t_copied, b // 2)
                        else:
                            pe.wait_ge(at_copied, b + 2)
                        transpose_hm(b - 1)
                    if u == 25 and not first:
                        if last:
                            pe.wait_ge(pq_copied, b + 1)
                        else:
                            pe.wait_ge(t_copied, b + 2)
                        layer0(b - 1, 1 - par)
                    if u == 30 and not last:
                        if first:
                            pe.wait_ge(t_copied, b + 2)
                        else:
                            pe.wait_ge(l0_added, b)
                        project_pq(b + 1, 1 - par)
                    if u == 34 and par == 0 and not last_pair:
                        if first:
                            pe.wait_ge(at_copied, b + 2)
                        else:
                            pe.wait_ge(hmt_copied, b)
                        transpose_xt(b // 2 + 1)
                    if u == 42 and par == 0 and not first:
                        if last_pair:
                            pe.wait_ge(hmt_copied, b)
                        else:
                            pe.wait_ge(xt_copied, b // 2 + 2)
                        transpose_x1(b // 2 - 1)
                    if u == 0:
                        pe.wait_ge(wq_loaded, 16 * WLOADS * (b + 1))
                        pe.wait_ge(mv_loaded, 16 * (b + 1))
                        pe.wait_ge(masks_made, b + 1)
                    if not (first and u < BANKS):
                        pe.wait_ge(dve_ind if u % 2 else act_ind, EU * b + u // 2 - 1)
                    difference(u, par)
                    if u == LAG:
                        pe.wait_ge(q_split, b + 1)
                        if not first:
                            pe.wait_ge(s_copied, 2 * b - 1)
                    if u == LAG + HALF_UNITS and not first:
                        pe.wait_ge(s_copied, 2 * b)
                    if u >= LAG:
                        contract(u - LAG, par)
                    elif not first:
                        contract(UNITS + u - LAG, 1 - par)

            graphs(pe, graph)
            pe.wait_ge(act_ind, EU * NB)
            pe.wait_ge(dve_ind, EU * NB)
            for u in range(UNITS - LAG, UNITS):
                contract(u, 1)
            pe.wait_ge(hmt_copied, NB - 1)
            transpose_hm(NB - 1)
            pe.wait_ge(l0_added, NB - 1)
            layer0(NB - 1, 1)
            transpose_x1(PAIRS - 1)

            pe.wait_ge(bn_ready, 1)
            nc.tensor.matmul(bx[:, 0:2], havg[:, :], bn_mv[:, :], start=True, stop=True)
            nc.tensor.matmul(bx[:, 2:3], hdif[:, :], bn_mv[:, 0:1], start=True, stop=True).then_inc(bn_comb, 1)
            pe.wait_ge(wbn_ready, 1)
            nc.tensor.matmul(by[:, 0:F], shift[:, :], lw[0:F], start=True, stop=False)
            nc.tensor.matmul(by[:, 0:F], ones[:, :], lb_row[:, :], start=False, stop=True).then_inc(e_psum, 1)

            def project_x(g):
                if g >= 2:
                    pe.wait_ge(xe_ready, g - 1)
                for k in range(GB // 2):
                    ins = nc.tensor.matmul(d_bank[g % 2][:, 2 * F * k:2 * F * k + 2 * F],
                                           x1t_all[:, GB // 2 * g + k], w_bn[:, :, :].rearrange("p a f -> p (a f)"),
                                           start=True, stop=True)
                ins.then_inc(xw_psum, 1)

            project_x(0)
            for g in range(GROUPS):
                if g + 1 < GROUPS:
                    project_x(g + 1)
                pe.wait_ge(ys_ready, g + 1)
                if g >= 2:
                    pe.wait_ge(zz_ready, g - 1)
                for k in range(GB):
                    ins = nc.tensor.matmul(d_bank[2 + g % 2][:, F * k:F * k + F], at_all[:, GB * g + k],
                                           ys[g % 2][:, k], start=True, stop=True)
                ins.then_inc(ay_psum, 1)


_INS = ["x", "adj", "L0_gnn_W1", "L0_gnn_b1", "L0_gnn_W2", "L0_gnn_b2",
        "L1_gnn_gamma", "L1_gnn_beta", "L1_gnn_W", "L1_gnn_b"]
_OUTS = [((64, 128, 64), "float32")]


def kernel(**inputs):
    import numpy as _np
    import concourse.bacc as _bacc
    from concourse import mybir as _mybir
    from concourse.bass_utils import run_bass_kernel_spmd as _run

    nc = _bacc.Bacc("TRN2", target_bir_lowering=False, num_devices=1)
    arrays, args = {}, []
    for name in _INS:
        a = _np.ascontiguousarray(inputs[name])
        arrays[f"in_{name}_dram"] = a
        args.append(nc.dram_tensor(f"in_{name}_dram", a.shape, _mybir.dt.from_np(a.dtype), kind="ExternalInput").ap())
    for i, (shape, dtype) in enumerate(_OUTS):
        dt = _mybir.dt.from_np(_np.dtype(dtype))
        args.append(nc.dram_tensor(f"out_{i}_dram", shape, dt, kind="ExternalOutput").ap())
    gnn_kernel(nc, *args)
    r = _run(nc, [arrays], core_ids=[0])
    return r.results[0]["out_0_dram"]
```

```python
import concourse.bass as bass
from concourse import mybir
from contextlib import ExitStack


def gnn_kernel(nc, x, adj, W1, b1, W2, b2, gamma, beta, W, bvec, out):
    f32, bf16 = mybir.dt.float32, mybir.dt.bfloat16
    ALU, ACT, AX = mybir.AluOpType, mybir.ActivationFunctionType, mybir.AxisListType

    NB, N, F = x.shape
    H = W1.shape[1]
    EPS = 1e-5
    HU = 4
    UNITS = H // HU
    SETS = 8
    C1, HQ = 3, 2
    HH = H // 2
    HALF_UNITS = UNITS // 2
    PARTS = 3
    PROWS, QROWS = PARTS, PARTS * HU
    QP0 = PROWS * SETS
    BANKS = 4
    LAG = 4
    RING = 4
    BIG = float(2 ** 60)
    PAIRS = NB // 2
    EU = UNITS // 2
    WLOADS, QSTORES = SETS, C1
    assert UNITS == SETS * C1 * HQ and N == 128 and 2 * F == 128

    ctx = ExitStack()
    with ctx:
        def sb(name, shape, dt=f32):
            return ctx.enter_context(nc.sbuf_tensor(name, shape, dt))

        def sem(name):
            return ctx.enter_context(nc.semaphore(name))

        GB = 8
        GROUPS = NB // GB

        wq = [sb(f"wq{i}", [128, C1, SETS, HQ, N]) for i in range(2)]
        mv = [sb(f"mv{i}", [128, HU, C1, HQ, N]) for i in range(2)]
        tparts = [sb(f"tparts{i}", [HH, PARTS, 2, HQ, N]) for i in range(2)]
        at_all = sb("at_all", [128, NB, N])
        at_raw = sb("at_raw", [128, N])
        at_less = sb("at_less", [128, N])
        x_all = sb("x_all", [128, NB, F])
        x1t_all = sb("x1t_all", [128, PAIRS, N])
        a_in = [sb(f"a_in{i}", [128, N]) for i in range(2)]
        x_in = sb("x_in", [128, 2, F])
        xt = sb("xt", [128, N])
        qn = [sb(f"qn{i}", [128, PARTS + 1, H]) for i in range(2)]
        pn = [sb(f"pn{i}", [128, H]) for i in range(2)]
        ind_a = [sb(f"ind_a{i}", [128, HU * N], bf16) for i in range(RING)]
        ind_v = [sb(f"ind_v{i}", [128, HU * N], bf16) for i in range(RING)]
        mask = [sb(f"mask{i}", [128, N], bf16) for i in range(2)]
        nmask = [sb(f"nmask{i}", [128, N], bf16) for i in range(2)]
        sums = [sb(f"sums{i}", [128, 2, PARTS + 1, HH]) for i in range(2)]
        hm = sb("hm", [128, 2, HH])
        hm_t = sb("hm_t", [HH, 2, N])
        d_now = [sb(f"d_now{i}", [128, 1]) for i in range(2)]
        rs_now = [sb(f"rs_now{i}", [128, 1]) for i in range(2)]
        x1 = sb("x1", [128, 2, F])
        ln_stats = sb("ln_stats", [128, 6])
        ln_mv = sb("ln_mv", [128, 2])
        ln_var = sb("ln_var", [128, 1])
        ln_rstd = sb("ln_rstd", [128, 1])
        eps = sb("eps", [128, GB])
        half_down = sb("half_down", [128, GB])
        ident = sb("ident", [128, 128])
        neg_big = sb("neg_big", [128, 128], bf16)
        pat_w = sb("pat_w", [128, SETS])
        pat_m = sb("pat_m", [128, HU])
        ones = sb("ones", [1, 128])
        w_raw = sb("w_raw", [128, 2, H])
        w_sign = sb("w_sign", [128, 2, H])
        w_diff = sb("w_diff", [128, 2, H])
        w_nat = [sb(f"w_nat{i}", [128, 2, H]) for i in range(2)]
        w_t = [sb(f"w_t{i}", [128, 2, HQ, HH]) for i in range(2)]
        b1_row = sb("b1_row", [1, H])
        b1_diff = sb("b1_diff", [1, H])
        b1_t = sb("b1_t", [1, HQ, HH])
        b2_row = sb("b2_row", [1, F])
        b1_all = sb("b1_all", [128, H])
        b1t_all = sb("b1t_all", [HH, HQ])
        b2_parts = sb("b2_parts", [128, PARTS, F])
        w2_sb = sb("w2_sb", [HH, 2, F])
        lw = sb("lw", [128, F])
        lb_row = sb("lb_row", [1, F])
        gb = sb("gb", [128, 2])
        havg = sb("havg", [128, 128])
        hdif = sb("hdif", [128, 128])
        bn_st = sb("bn_st", [128, 8, 6])
        bn_mv = sb("bn_mv", [128, 2])
        bn = sb("bn", [128, 8])
        w_bn = sb("w_bn", [128, 2, F])
        shift = sb("shift", [F, PARTS])
        e_parts = sb("e_parts", [PARTS, PARTS, F])
        e_sel = sb("e_sel", [PARTS, F])
        ones_bf = sb("ones_bf", [PARTS, N], bf16)
        nsd_all = sb("nsd_all", [128, NB])
        l1_tiles = [t[:, :, :, :, :].rearrange("p c s q k -> p (c s q k)").rearrange(
            "p (t b f) -> p t b f", b=GB, f=F) for t in wq]
        xe, zz = ([l1_tiles[i][:, g] for g in range(GROUPS)] for i in range(2))
        g_st = [sb(f"g_st{i}", [128, GB, 6]) for i in range(2)]
        g_mv = [sb(f"g_mv{i}", [128, GB, 2]) for i in range(2)]
        g_scale = [sb(f"g_scale{i}", [128, GB]) for i in range(2)]
        g_shift = [sb(f"g_shift{i}", [128, GB]) for i in range(2)]

        d_bank = [ctx.enter_context(nc.psum_tensor(f"d_bank{i}", [128, 512], f32)) for i in range(BANKS)]
        s_bank = [ctx.enter_context(nc.psum_tensor(f"s_bank{i}", [128, 512], f32)) for i in range(2)]
        bx = ctx.enter_context(nc.psum_tensor("bx", [128, 512], f32))
        by = ctx.enter_context(nc.psum_tensor("by", [128, 512], f32))

        x_bank = [d_bank[0], d_bank[1], s_bank[0], s_bank[1]]
        a_bank = [d_bank[2], d_bank[3], bx, by]

        q_dram = [nc.dram_tensor(f"q_scratch{i}", (SETS, HU, PARTS, C1, HQ * N), f32, kind="Internal").ap()
                  for i in range(2)]
        p_dram = [nc.dram_tensor(f"p_scratch{i}", (PARTS, HH, HQ * N), f32, kind="Internal").ap()
                  for i in range(2)]

        w1_in, w2_in, b_in, l1_in, x_all_in = (sem(n) for n in ("w1_in", "w2_in", "b_in", "l1_in", "x_all_in"))
        a_loaded, x_loaded = [sem(f"a_loaded{i}") for i in range(2)], sem("x_loaded")
        pool_step, dve_step, act_setup = sem("pool_step"), sem("dve_step"), sem("act_setup")
        pats_ready, ident_ready, weights_ready = sem("pats_ready"), sem("ident_ready"), sem("weights_ready")
        bias_psum, bias_ready, qn_ones = sem("bias_psum"), sem("bias_ready"), sem("qn_ones")
        operands_init = sem("operands_init")
        xt_psum, xt_copied = sem("xt_psum"), sem("xt_copied")
        at_psum, at_copied = sem("at_psum"), sem("at_copied")
        t_psum, t_copied, tq_split, tp_split = (sem(n) for n in ("t_psum", "t_copied", "tq_split", "tp_split"))
        pq_psum, pq_copied, q_split = sem("pq_psum"), sem("pq_copied"), sem("q_split")
        q_stored, p_stored = sem("q_stored"), sem("p_stored")
        wq_loaded, mv_loaded = sem("wq_loaded"), sem("mv_loaded")
        d_done, masks_made = sem("d_done"), sem("masks_made")
        d_for_act, d_for_dve = sem("d_for_act"), sem("d_for_dve")
        act_ind, dve_ind, contracted = sem("act_ind"), sem("dve_ind"), sem("contracted")
        s_copied, hm_step, hm_ready = sem("s_copied"), sem("hm_step"), sem("hm_ready")
        hmt_psum, hmt_copied, l0_psum, l0_added = (sem(n) for n in ("hmt_psum", "hmt_copied", "l0_psum", "l0_added"))
        ln_step, x1_ready, x1_kept = sem("ln_step"), sem("x1_ready"), sem("x1_kept")
        x1t_psum, x1t_copied = sem("x1t_psum"), sem("x1t_copied")
        t_step, q_step, pow_consts = sem("t_step"), sem("q_step"), sem("pow_consts")
        var_ready, rstd_step, rstd_ready = sem("var_ready"), sem("rstd_step"), sem("rstd_ready")
        bn_var, bn_rstd = sem("bn_var"), sem("bn_rstd")
        stats_made, bn_ready, bn_comb, wbn_ready, e_psum = sem("stats_made"), sem("bn_ready"), sem("bn_comb"), sem("wbn_ready"), sem("e_psum")
        shift_ready, e_ready = sem("shift_ready"), sem("e_ready")
        rs_ready, less_ready, at_scaled = sem("rs_ready"), sem("less_ready"), sem("at_scaled")
        nsd_made = sem("nsd_made")
        xw_psum, xe_ready, ax_psum = sem("xw_psum"), sem("xe_ready"), sem("ax_psum")
        zz_ready, zl_ready = sem("zz_ready"), sem("zl_ready")
        y2_ready, g_mv_ready = sem("y2_ready"), sem("g_mv_ready")
        g_step, g_ready, yf_ready = sem("g_step"), sem("g_ready"), sem("yf_ready")
        out_stored = sem("out_stored")

        block = ctx.enter_context(nc.Block())

        def hi(ap):
            return ap.bitcast(bf16)

        def graphs(eng, program):
            program(0, 0, True, False)
            program(1, 1, False, False)
            with eng.Fori(1, PAIRS - 1) as pair:
                program(2 * pair, 0, False, False)
                program(2 * pair + 1, 1, False, False)
            program(NB - 2, 0, False, False, True)
            program(NB - 1, 1, False, True, True)

        @block.sync
        def _(sp):
            sp.dma_start(x_in[:, :, :], x[0:2].rearrange("b j f -> j b f")).then_inc(x_loaded, 16)
            w1_v = W1.rearrange("(t f) h -> f t h", t=2)
            sp.dma_start(w_raw[0:F], w1_v).then_inc(w1_in, 16)
            sp.dma_start(w_raw[F:128], w1_v).then_inc(w1_in, 16)
            sp.dma_start(b1_row[:, :], b1.rearrange("(a h) -> a h", a=1)).then_inc(b_in, 16)
            sp.dma_start(b2_row[:, :], b2.rearrange("(a h) -> a h", a=1)).then_inc(b_in, 16)
            sp.dma_start(lb_row[:, :], bvec.rearrange("(a h) -> a h", a=1)).then_inc(b_in, 16)
            for i in range(2):
                sp.dma_start(a_in[i][:, :], adj[i]).then_inc(a_loaded[i], 16)
            sp.dma_start(w2_sb[:, :, :], W2.rearrange("(t h) o -> h t o", t=2)).then_inc(w2_in, 16)
            for i in range(2):
                rows = slice(F * i, F * i + F)
                sp.dma_start(lw[rows], W).then_inc(l1_in, 16)
                sp.dma_start(gb[rows, 0:1], gamma.rearrange("(c a) -> c a", a=1)).then_inc(l1_in, 16)
                sp.dma_start(gb[rows, 1:2], beta.rearrange("(c a) -> c a", a=1)).then_inc(l1_in, 16)
            sp.dma_start(x_all[:, :, :], x.rearrange("b j f -> j b f")).then_inc(x_all_in, 16)

            def value(v):
                if isinstance(v, int):
                    return v
                reg = sp.alloc_register()
                sp.reg_mov(reg, v)
                return sp.snap(reg, donate=True)

            def counts(n):
                return {"parts": value(n + 1), "wq_before": value(16 * WLOADS * (n - 1)),
                        "mv_before": value(16 * (n - 1)), "d_before": value(EU * (n - 1)),
                        "q_stored": value(16 * QSTORES * (n + 1)), "p_stored": value(16 * (n + 1))}

            def operands(cnt, par, first_use):
                sp.wait_ge(tq_split, cnt["parts"])
                if not first_use:
                    sp.wait_ge(wq_loaded, cnt["wq_before"])
                    sp.wait_ge(mv_loaded, cnt["mv_before"])
                for c1 in range(C1):
                    sp.dma_start(q_dram[par][:, :, :, c1].rearrange("s h i k -> (s h) i k"),
                                 tparts[par][c1:HH:C1, :, 1].rearrange("p i q k -> p i (q k)")).then_inc(q_stored, 16)
                sp.wait_ge(tp_split, cnt["parts"])
                sp.dma_start(p_dram[par].rearrange("i t k -> t i k"),
                             tparts[par][:, :, 0].rearrange("p i q k -> p i (q k)")).then_inc(p_stored, 16)
                if first_use:
                    sp.wait_ge(operands_init, 4)
                else:
                    sp.wait_ge(d_for_dve, cnt["d_before"])
                sp.wait_ge(q_stored, cnt["q_stored"])
                for s in range(SETS):
                    sp.dma_start(wq[par][QP0 + s:QP0 + SETS * QROWS:SETS, :, s].rearrange("r c q k -> r c (q k)"),
                                 q_dram[par][s].rearrange("h i c k -> (h i) c k")).then_inc(wq_loaded, 16)
                sp.wait_ge(p_stored, cnt["p_stored"])
                sp.dma_start(mv[par][0:QP0].rearrange("p h c q k -> p (h c q k)"),
                             p_dram[par].rearrange("i (s m) k -> (i s) (m k)", s=SETS)).then_inc(mv_loaded, 16)

            operands(counts(0), 0, True)

            def graph(b, par, first, last, last_pair=False):
                ahead, done, pairs_done = value(b + 2), value(b + 1), value(b // 2 + 1)
                cnt = counts(b + 1)
                if not last_pair:
                    sp.wait_ge(at_psum, done)
                    sp.wait_ge(d_done, done)
                    sp.dma_start(a_in[par][:, :], adj[bass.ds(ahead, 1)].rearrange("a j k -> (a j) k"))\
                        .then_inc(a_loaded[par], 16)
                if par == 0 and not last_pair:
                    sp.wait_ge(xt_psum, pairs_done)
                    sp.dma_start(x_in[:, :, :], x[bass.ds(ahead, 2)].rearrange("b j f -> j b f"))\
                        .then_inc(x_loaded, 16)
                if not last:
                    operands(cnt, 1 - par, first)

            graphs(sp, graph)

            for g in range(GROUPS):
                sp.wait_ge(yf_ready, g + 1)
                sp.dma_start(out[GB * g:GB * g + GB].rearrange("b j o -> j b o"), x_all[:, GB * g:GB * g + GB])\
                    .then_inc(out_stored, 16)
            sp.wait_ge(out_stored, 16 * GROUPS)

        @block.gpsimd
        def _(pool):
            steps = [0]

            def link(ins):
                steps[0] += 1
                ins.then_inc(pool_step, 1)
                pool.wait_ge(pool_step, steps[0])

            nc.gpsimd.memset(eps[:, :], EPS).then_inc(pow_consts, 1)
            nc.gpsimd.memset(half_down[:, :], -0.5).then_inc(pow_consts, 1)
            link(nc.gpsimd.memset(pat_w[:, :], 0.0))
            for i in range(PROWS):
                link(nc.gpsimd.affine_select(out=pat_w[:, :], in_=pat_w[:, :], compare_op=ALU.not_equal, fill=1.0,
                                             base=-SETS * i, pattern=[[-1, SETS]], channel_multiplier=1))
            rows = SETS * PARTS
            link(nc.gpsimd.memset(pat_m[:, :], 1.0))
            link(nc.gpsimd.affine_select(out=pat_m[:, :], in_=pat_m[:, :], compare_op=ALU.is_ge, fill=0.0,
                                         base=-QP0, pattern=[[-rows, HU]], channel_multiplier=1))
            nc.gpsimd.affine_select(out=pat_m[:, :], in_=pat_m[:, :], compare_op=ALU.is_ge, fill=0.0,
                                    base=QP0 + rows - 1, pattern=[[rows, HU]], channel_multiplier=-1)\
                .then_inc(pats_ready, 1)
            link(nc.gpsimd.memset(ident[:, :], 0.0))
            nc.gpsimd.affine_select(out=ident[:, :], in_=ident[:, :], compare_op=ALU.not_equal, fill=1.0,
                                    base=0, pattern=[[-1, 128]], channel_multiplier=1).then_inc(ident_ready, 1)
            for i in range(2):
                nc.gpsimd.memset(qn[i][:, PARTS], 1.0).then_inc(qn_ones, 1)

            def split_t(n, par):
                for t in (1, 0):
                    pool.wait_ge(t_copied, 2 * n + 2 - t)
                    for i in range(1, PARTS):
                        part = tparts[par][:, i, t].rearrange("p q k -> p (q k)")
                        before = tparts[par][:, i - 1, t].rearrange("p q k -> p (q k)")
                        if i == 2:
                            pool.wait_ge(t_step, 2 * n + (1 if t else 2))
                        nc.gpsimd.tensor_tensor(part, before, hi(before)[:, 1::2], ALU.subtract)\
                            .then_inc(t_step if i == 1 else tq_split if t else tp_split, 1)

            def split_q(n, par):
                pool.wait_ge(pq_copied, n + 1)
                nc.gpsimd.tensor_tensor(pn[par][:, :], pn[par][:, :], b1_all[:, :], ALU.add).then_inc(q_step, 1)
                for i in range(1, PARTS):
                    t = qn[par]
                    if i == 2:
                        pool.wait_ge(q_step, 2 * n + 2)
                    nc.gpsimd.tensor_tensor(t[:, i], t[:, i - 1], hi(t[:, i - 1])[:, 1::2], ALU.subtract)\
                        .then_inc(q_step if i == 1 else q_split, 1)

            def degree_power(n, par):
                pool.wait_ge(d_done, n + 1)
                nc.gpsimd.tensor_tensor(rs_now[par][:, :], d_now[par][:, :], half_down[:, 0:1], ALU.pow)\
                    .then_inc(rs_ready, 1)

            def subtract_identity(n):
                pool.wait_ge(at_copied, n + 1)
                if not (isinstance(n, int) and n == 0):
                    pool.wait_ge(at_scaled, n)
                nc.gpsimd.tensor_tensor(at_less[:, :], at_raw[:, :], ident[:, :], ALU.subtract)\
                    .then_inc(less_ready, 1)

            def finish_hm(o, par, first):
                pool.wait_ge(s_copied, 2 * o + 2)
                if not first:
                    pool.wait_ge(hmt_psum, o)
                nc.gpsimd.tensor_tensor(hm[:, :, :], pn[par][:, :].rearrange("p (t h) -> p t h", t=2),
                                        sums[par][:, :, PARTS], ALU.mult).then_inc(hm_step, 1)
                for i in range(PARTS):
                    pool.wait_ge(hm_step, PARTS * o + i + 1)
                    nc.gpsimd.tensor_tensor(hm[:, :, :], hm[:, :, :], sums[par][:, :, i], ALU.subtract)\
                        .then_inc(hm_ready if i == PARTS - 1 else hm_step, 1)

            def rstd(o):
                pool.wait_ge(var_ready, o + 1)
                nc.gpsimd.tensor_tensor(ln_var[:, :], ln_mv[:, 1:2], eps[:, 0:1], ALU.add).then_inc(rstd_step, 1)
                pool.wait_ge(rstd_step, o + 1)
                nc.gpsimd.tensor_tensor(ln_rstd[:, :], ln_var[:, :], half_down[:, 0:1], ALU.pow)\
                    .then_inc(rstd_ready, 1)

            pool.wait_ge(pow_consts, 2)
            pool.wait_ge(bias_ready, 1)
            split_t(0, 0)
            degree_power(0, 0)
            subtract_identity(0)
            split_q(0, 0)

            def graph(b, par, first, last, last_pair=False):
                if not last:
                    split_t(b + 1, 1 - par)
                    degree_power(b + 1, 1 - par)
                if not first:
                    finish_hm(b - 1, 1 - par, isinstance(b, int) and b == 1)
                if not last:
                    subtract_identity(b + 1)
                if not first:
                    rstd(b - 1)
                if not last:
                    split_q(b + 1, 1 - par)
                if par == 0 and not first:
                    keep_x1(b)
            def keep_x1(b):
                pool.wait_ge(x1_ready, b)
                pool_copy = nc.gpsimd.tensor_copy(x_all[:, bass.ds(b - 2, 2)], x1[:, :, :])
                pool_copy.then_inc(x1_kept, 1)

            graphs(pool, graph)
            finish_hm(NB - 1, 1, False)
            rstd(NB - 1)
            keep_x1(NB)

            pool.wait_ge(bn_var, 1)
            nc.gpsimd.tensor_tensor(bn[:, 4:5], bn[:, 3:4], half_down[:, 0:1], ALU.pow).then_inc(bn_rstd, 1)

            def add_x(g):
                pool.wait_ge(zl_ready, g + 1)
                if g == 0:
                    pool.wait_ge(x1_kept, PAIRS)
                nc.gpsimd.tensor_tensor(x_all[:, GB * g:GB * g + GB], zz[g], x_all[:, GB * g:GB * g + GB], ALU.add)\
                    .then_inc(y2_ready, 1)

            def scale_shift(g):
                i = g % 2
                pool.wait_ge(g_mv_ready, g + 1)
                if g >= 2:
                    pool.wait_ge(yf_ready, g - 1)
                nc.gpsimd.tensor_tensor(g_scale[i][:, :], g_mv[i][:, :, 1], half_down[:, 0:GB], ALU.pow)\
                    .then_inc(g_step, 1)
                pool.wait_ge(g_step, g + 1)
                nc.gpsimd.tensor_tensor(g_shift[i][:, :], g_mv[i][:, :, 0], g_scale[i][:, :], ALU.mult)\
                    .then_inc(g_ready, 1)

            for g in range(GROUPS + 1):
                if g < GROUPS:
                    add_x(g)
                if g >= 1:
                    scale_shift(g - 1)

        @block.scalar
        def _(act):
            act.wait_ge(pats_ready, 1)
            nc.scalar.activation(mv[0][:, :, :, :, :].rearrange("p h c q k -> p h (c q k)"),
                                 pat_m[:, :].unsqueeze(2).broadcast_to([128, HU, C1 * HQ * N]), ACT.Copy)\
                .then_inc(operands_init, 1)
            nc.scalar.activation(mv[1][:, :, :, :, :].rearrange("p h c q k -> p h (c q k)"),
                                 pat_m[:, :].unsqueeze(2).broadcast_to([128, HU, C1 * HQ * N]), ACT.Copy)\
                .then_inc(operands_init, 1)

            def copy_xt(pair):
                act.wait_ge(xt_psum, pair + 1)
                nc.scalar.activation(xt[:, :], by[:, 0:N], ACT.Copy).then_inc(xt_copied, 1)

            def copy_t_q(n, par, first_use):
                act.wait_ge(t_psum, n + 1)
                if not first_use:
                    act.wait_ge(q_stored, 16 * QSTORES * (n - 1))
                    act.wait_ge(p_stored, 16 * (n - 1))
                nc.scalar.activation(tparts[par][:, 0, 1].rearrange("p q k -> p (q k)"),
                                     bx[0:HH, HQ * N:2 * HQ * N], ACT.Copy).then_inc(t_copied, 1)

            def copy_t_p(par):
                for q in range(HQ):
                    ins = nc.scalar.activation(tparts[par][:, 0, 0, q], bx[0:HH, N * q:N * q + N], ACT.Identity,
                                               bias=b1t_all[:, q:q + 1])
                ins.then_inc(t_copied, 1)

            def copy_at(n, first_use):
                act.wait_ge(at_psum, n + 1)
                if not first_use:
                    act.wait_ge(masks_made, n)
                    act.wait_ge(less_ready, n)
                nc.scalar.activation(at_raw[:, :], by[:, 0:N], ACT.Copy).then_inc(at_copied, 1)

            def scale_at(n, par):
                act.wait_ge(less_ready, n + 1)
                act.wait_ge(rs_ready, n + 1)
                nc.scalar.activation(at_all[:, bass.ds(n, 1)].rearrange("p a k -> p (a k)"), at_less[:, :],
                                     ACT.Identity, scale=rs_now[par][:, 0:1]).then_inc(at_scaled, 1)

            def copy_pq(n, par, first_use):
                act.wait_ge(pq_psum, n + 1)
                if not first_use:
                    act.wait_ge(contracted, UNITS * (n - 1))
                    act.wait_ge(hm_ready, n - 1)
                nc.scalar.activation(pn[par][:, :], bx[:, 0:H], ACT.Copy)
                nc.scalar.activation(qn[par][:, 0], bx[:, H:2 * H], ACT.Copy).then_inc(pq_copied, 1)

            def copy_sums(b, par, half, first_use):
                act.wait_ge(contracted, UNITS * b + HALF_UNITS * (half + 1))
                if not first_use and half == 0:
                    act.wait_ge(hm_ready, b - 1)
                nc.scalar.activation(sums[par][:, half].rearrange("p i h -> p (i h)"),
                                     s_bank[half][:, 0:(PARTS + 1) * HH], ACT.Copy).then_inc(s_copied, 1)

            def copy_hmt(o, first_use):
                act.wait_ge(hmt_psum, o + 1)
                if not first_use:
                    act.wait_ge(l0_psum, o)
                nc.scalar.activation(hm_t[:, :, :].rearrange("p t k -> p (t k)"), by[0:HH, 0:2 * N], ACT.Copy)\
                    .then_inc(hmt_copied, 1)

            def copy_x1t(pair):
                act.wait_ge(x1t_psum, pair + 1)
                nc.scalar.activation(x1t_all[:, bass.ds(pair, 1)].rearrange("p a k -> p (a k)"), by[:, 0:N], ACT.Copy)\
                    .then_inc(x1t_copied, 1)

            copy_xt(0)
            act.wait_ge(bias_ready, 1)
            copy_t_q(0, 0, True)
            copy_t_p(0)
            copy_at(0, True)
            copy_pq(0, 0, True)
            nc.scalar.preload_act_table(ACT.Sigmoid)

            def graph(b, par, first, last, last_pair=False):
                for v in range(EU):
                    act.wait_ge(d_for_act, EU * b + v + 1)
                    if not (first and v < RING):
                        act.wait_ge(contracted, UNITS * b + 2 * (v - RING) + 1)
                    nc.scalar.activation(ind_a[v % RING][:, :], d_bank[2 * v % BANKS][:, :], ACT.Sigmoid, scale=BIG)\
                        .then_inc(act_ind, 1)
                    if v == 0 and not last:
                        copy_t_q(b + 1, 1 - par, first)
                    if v == 1 and not last:
                        copy_t_p(1 - par)
                    if v == 3 and not first:
                        copy_sums(b - 1, 1 - par, 1, True)
                    if v == 5 and not last:
                        copy_at(b + 1, False)
                    if v == 9 and first:
                        scale_at(0, 0)
                    if v == 21 and not last:
                        scale_at(b + 1, 1 - par)
                    if v == 11 and not first:
                        copy_hmt(b - 1, isinstance(b, int) and b == 1)
                    if v == 14:
                        copy_sums(b, par, 0, isinstance(b, int) and b < 2)
                    if v == 17 and not last:
                        copy_pq(b + 1, 1 - par, first)
                    if v == 19 and par == 0 and not last_pair:
                        copy_xt(b // 2 + 1)
                    if v == 23 and par == 0 and not first:
                        copy_x1t(b // 2 - 1)

            graphs(act, graph)
            copy_sums(NB - 1, 1, 1, True)
            copy_hmt(NB - 1, False)
            copy_x1t(PAIRS - 1)

            def copy_xe(g):
                act.wait_ge(xw_psum, g + 1)
                nc.scalar.activation(xe[g].rearrange("p b f -> p (b f)"), x_bank[g % 4][:, :], ACT.Copy)\
                    .then_inc(xe_ready, 1)

            def normalise(g):
                act.wait_ge(g_ready, g + 1)
                for k in range(GB):
                    y = x_all[:, GB * g + k]
                    ins = nc.scalar.activation(y, y, ACT.Identity, bias=g_shift[g % 2][:, k:k + 1],
                                               scale=g_scale[g % 2][:, k:k + 1])
                ins.then_inc(yf_ready, 1)

            AHEAD = 5
            for g in range(AHEAD):
                copy_xe(g)
            for g in range(GROUPS):
                if g + AHEAD < GROUPS:
                    copy_xe(g + AHEAD)
                normalise(g)

        @block.vector
        def _(dve):
            steps = [0]

            def link(ins):
                steps[0] += 1
                ins.then_inc(dve_step, 1)
                dve.wait_ge(dve_step, steps[0])

            link(nc.vector.memset(ones[:, :], 1.0))
            link(nc.vector.memset(ones_bf[:, :], 1.0))
            for i in range(2):
                link(nc.vector.memset(w_nat[i][:, :, :], 0.0))
                link(nc.vector.memset(w_t[i][:, :, :, :], 0.0))
            link(nc.vector.memset(w_bn[:, :, :], 0.0))
            dve.wait_ge(w1_in, 32)
            link(nc.vector.tensor_tensor(w_sign[:, 0], w_raw[:, 0], w_raw[:, 1], ALU.add))
            link(nc.vector.tensor_scalar(w_sign[:, 1], w_raw[:, 1], -1.0, None, ALU.mult))
            dve.wait_ge(b_in, 48)
            link(nc.vector.tensor_copy(w_diff[:, :, :], w_sign[:, :, :]))
            link(nc.vector.tensor_copy(b1_diff[:, :], b1_row[:, :]))

            def even_units(ap, a, b):
                return ap.rearrange("p (v k h) -> p v k h", k=2, h=HU)[:, a:b, 0]

            for dst, src in ((w_diff[:, 0], w_sign[:, 0]), (w_diff[:, 1], w_sign[:, 1]),
                             (b1_diff[:, :], b1_row[:, :])):
                link(nc.vector.tensor_tensor(even_units(dst, BANKS // 2, EU), even_units(src, BANKS // 2, EU),
                                             even_units(src, 0, EU - BANKS // 2), ALU.subtract))

            def reorder(dst, src):
                for q in range(HQ):
                    ins = nc.vector.tensor_copy(
                        dst[:, q].rearrange("p (m c) -> p c m", c=C1),
                        src.rearrange("p (c q m) -> p c q m", c=C1, q=HQ)[:, :, q])
                return ins

            for i in range(2):
                rows = slice(F * i, F * i + F)
                link(nc.vector.tensor_copy(w_nat[i][rows, 0], w_sign[rows, 0]))
                link(nc.vector.tensor_copy(w_nat[i][rows, 1], w_raw[rows, 1]))
                for t in range(2):
                    link(reorder(w_t[i][rows, t], w_diff[rows, t]))
            reorder(b1_t[:, :, :], b1_diff[:, :]).then_inc(weights_ready, 1)
            dve.wait_ge(ident_ready, 1)
            nc.vector.tensor_scalar(neg_big[:, :], ident[:, :], -BIG, None, ALU.mult).then_inc(weights_ready, 1)
            dve.wait_ge(bias_psum, 1)
            link(nc.vector.tensor_copy(b1_all[:, :], by[:, 0:H]))
            link(nc.vector.tensor_copy(b2_parts[:, 0], by[:, H:H + F]))
            for i in range(1, PARTS):
                link(nc.vector.tensor_tensor(b2_parts[:, i], b2_parts[:, i - 1], hi(b2_parts[:, i - 1])[:, 1::2],
                                             ALU.subtract))
            nc.vector.tensor_copy(b1t_all[:, :], bx[0:HH, 0:HQ])\
                .then_inc(bias_ready, 1)

            def degree(n, par):
                dve.wait_ge(a_loaded[par], 16 * (n // 2 + 1))
                nc.vector.tensor_reduce(d_now[par][:, :], a_in[par][:, :], AX.X, ALU.add).then_inc(d_done, 1)

            def make_masks(n, par):
                dve.wait_ge(at_copied, n + 1)
                at = at_raw[:, :]
                nc.vector.tensor_scalar(mask[par][:, :], at, 0.0, None, ALU.is_gt)
                nc.vector.tensor_scalar(nmask[par][:, :], at, 0.0, None, ALU.is_le).then_inc(masks_made, 1)

            def negative_root(n, par):
                dve.wait_ge(rs_ready, n + 1)
                nc.vector.scalar_tensor_tensor(out=nsd_all[:, bass.ds(n, 1)], in0=d_now[par][:, :], scalar=-1.0,
                                               in1=rs_now[par][:, :], op0=ALU.mult, op1=ALU.mult)\
                    .then_inc(nsd_made, 1)

            def norm_step(o, par, k):
                xo = x_all[:, bass.ds(o, 1)].rearrange("p a f -> p (a f)")
                if k == 0:
                    dve.wait_ge(l0_psum, o + 1)
                    if par == 0 and not (isinstance(o, int) and o == 0):
                        dve.wait_ge(x1_kept, o // 2)
                        dve.wait_ge(x1t_psum, o // 2)
                    nc.vector.tensor_tensor(x1[:, par], xo, bx[:, 0:F], ALU.add).then_inc(l0_added, 1)
                elif k == 1:
                    dve.wait_ge(l0_added, o + 1)
                    nc.vector.bn_stats(ln_stats[:, :], x1[:, par]).then_inc(ln_step, 1)
                elif k == 2:
                    nc.vector.bn_aggr(ln_mv[:, :], ln_stats[:, :]).then_inc(var_ready, 1)
                elif k == 3:
                    dve.wait_ge(rstd_ready, o + 1)
                    nc.vector.tensor_scalar(x1[:, par], x1[:, par], ln_mv[:, 0:1], ln_rstd[:, 0:1],
                                            ALU.subtract, ALU.mult).then_inc(x1_ready, 1)

            for i in range(2):
                dve.wait_ge(pats_ready, 1)
                nc.vector.tensor_copy(wq[i][:, :, :, :, :].rearrange("p c s q k -> p c s (q k)"),
                                      pat_w[:, :].unsqueeze(1).unsqueeze(3).broadcast_to([128, C1, SETS, HQ * N]))\
                    .then_inc(operands_init, 1)
                if i == 0:
                    degree(0, 0)
                    make_masks(0, 0)
                    negative_root(0, 0)
            dve.wait_ge(x_all_in, 16)

            def graph(b, par, first, last, last_pair=False):
                for w in range(EU):
                    if w == 16 and not first:
                        dve.wait_ge(ln_step, b)
                    dve.wait_ge(d_for_dve, EU * b + w + 1)
                    if not (first and w < RING):
                        dve.wait_ge(contracted, UNITS * b + 2 * (w - RING) + 2)
                    nc.vector.scalar_tensor_tensor(
                        out=ind_v[w % RING][:, :].rearrange("p (h k) -> p h k", k=N),
                        in0=d_bank[(2 * w + 1) % BANKS][:, :].rearrange("p (h k) -> p h k", k=N), scalar=0.0,
                        in1=mask[par][:, :].unsqueeze(1).broadcast_to([128, HU, N]),
                        op0=ALU.is_gt, op1=ALU.mult).then_inc(dve_ind, 1)
                    if w == 2 and not last:
                        degree(b + 1, 1 - par)
                    if w in (14, 15, 16, 19) and not first:
                        norm_step(b - 1, 1 - par, min(w - 14, 3))
                    if w == 18 and not last:
                        make_masks(b + 1, 1 - par)
                    if w == 21 and not last:
                        negative_root(b + 1, 1 - par)
                    if last_pair and w % 6 == 5 and (w // 6 < 3 or last):
                        chunk_stats(4 * par + w // 6 - par)

            def chunk_stats(i):
                w = PAIRS * N // 8
                dve.wait_ge(x1t_copied, (i + 1) * PAIRS // 8)
                nc.vector.bn_stats(bn_st[:, i], x1t_all[:, :, :].rearrange("p a k -> p (a k)")[:, w * i:w * i + w])\
                    .then_inc(stats_made, 1)

            graphs(dve, graph)
            link(nc.vector.memset(havg[:, :], 0.0))
            link(nc.vector.memset(hdif[:, :], 0.0))
            for i in range(2):
                for j in range(2):
                    r, c = slice(F * i, F * i + F), slice(F * j, F * j + F)
                    src = ident[r, r]
                    link(nc.vector.tensor_scalar(havg[r, c], src, 0.5, None, ALU.mult))
                    link(nc.vector.tensor_scalar(hdif[r, c], src, -0.5 if i else 0.5, None, ALU.mult))
            for k in range(4):
                if k == 2:
                    dve.wait_ge(ln_step, NB)
                norm_step(NB - 1, 1, k)

            chunk_stats(7)
            dve.wait_ge(stats_made, 8)
            nc.vector.bn_aggr(bn_mv[:, :], bn_st[:, :, :].rearrange("p a b -> p (a b)")).then_inc(bn_ready, 1)
            dve.wait_ge(bn_comb, 1)
            link(nc.vector.tensor_copy(bn[:, 0:3], bx[:, 0:3]))
            link(nc.vector.tensor_tensor(bn[:, 3:4], bn[:, 2:3], bn[:, 2:3], ALU.mult))
            nc.vector.tensor_scalar(bn[:, 3:4], bn[:, 3:4], bn[:, 1:2], EPS, ALU.add, ALU.add).then_inc(bn_var, 1)
            dve.wait_ge(bn_rstd, 1)
            dve.wait_ge(l1_in, 96)
            link(nc.vector.tensor_tensor(bn[:, 5:6], bn[:, 4:5], gb[:, 0:1], ALU.mult))
            for i in range(2):
                r = slice(F * i, F * i + F)
                ins = nc.vector.tensor_scalar(w_bn[r, i], lw[r], bn[r, 5:6], None, ALU.mult)
            ins.then_inc(wbn_ready, 1)
            link(nc.vector.tensor_tensor(bn[:, 6:7], bn[:, 0:1], bn[:, 5:6], ALU.mult))
            link(nc.vector.tensor_tensor(bn[:, 7:8], gb[:, 1:2], bn[:, 6:7], ALU.subtract))
            nc.vector.tensor_copy(shift[:, :], bn[0:F, 7:8].broadcast_to([F, PARTS])).then_inc(shift_ready, 1)
            dve.wait_ge(e_psum, 1)
            link(nc.vector.tensor_copy(e_parts[:, 0], by[0:PARTS, 0:F]))
            for i in range(1, PARTS):
                link(nc.vector.tensor_tensor(e_parts[:, i], e_parts[:, i - 1], hi(e_parts[:, i - 1])[:, 1::2],
                                             ALU.subtract))
            link(nc.vector.tensor_scalar(e_sel[:, :], e_parts[:, 0], ident[0:PARTS, 0:1], None, ALU.mult))
            for i in range(1, PARTS):
                ins = nc.vector.scalar_tensor_tensor(out=e_sel[:, :], in0=e_parts[:, i], scalar=ident[0:PARTS, i:i + 1],
                                                     in1=e_sel[:, :], op0=ALU.mult, op1=ALU.add)
                if i < PARTS - 1:
                    link(ins)
            ins.then_inc(e_ready, 1)

            def grouped(bank):
                return bank[:, :].rearrange("p (b f) -> p b f", f=F)

            def scale_ax(g):
                dve.wait_ge(ax_psum, g + 1)
                if g == 0:
                    dve.wait_ge(nsd_made, NB)
                nc.vector.tensor_tensor(zz[g], grouped(a_bank[g % 4]),
                                        nsd_all[:, GB * g:GB * g + GB].unsqueeze(2).broadcast_to([128, GB, F]),
                                        ALU.mult).then_inc(zz_ready, 1)

            def leaky(g):
                dve.wait_ge(zz_ready, g + 1)
                nc.vector.scalar_tensor_tensor(out=zz[g], in0=zz[g], scalar=0.01, in1=zz[g],
                                               op0=ALU.mult, op1=ALU.max).then_inc(zl_ready, 1)

            def stats(g):
                i = g % 2
                dve.wait_ge(y2_ready, g + 1)
                for k in range(GB):
                    ins = nc.vector.bn_stats(g_st[i][:, k], x_all[:, GB * g + k])
                link(ins)
                if g >= 2:
                    dve.wait_ge(g_ready, g - 1)
                for k in range(GB):
                    ins = nc.vector.bn_aggr(g_mv[i][:, k], g_st[i][:, k])
                link(ins)
                nc.vector.tensor_scalar(g_mv[i][:, :, 0], g_mv[i][:, :, 0], -1.0, None, ALU.mult)
                nc.vector.tensor_scalar(g_mv[i][:, :, 1], g_mv[i][:, :, 1], EPS, None, ALU.add).then_inc(g_mv_ready, 1)

            for g in range(GROUPS + 1):
                if g < GROUPS:
                    scale_ax(g)
                    leaky(g)
                if g >= 1:
                    stats(g - 1)

        @block.tensor
        def _(pe):
            def transpose_xt(pair):
                pe.wait_ge(x_loaded, 16 * (pair + 1))
                nc.tensor.transpose(by[:, 0:N], x_in[:, :, :].rearrange("p b f -> p (b f)"), ident[:, :])\
                    .then_inc(xt_psum, 1)

            def transpose_at(n, par):
                pe.wait_ge(a_loaded[par], 16 * (n // 2 + 1))
                nc.tensor.transpose(by[:, 0:N], a_in[par][:, :], ident[:, :]).then_inc(at_psum, 1)

            def project_t(n, par):
                for t in range(2):
                    for q in range(HQ):
                        k = (HQ * t + q) * N
                        ins = nc.tensor.matmul(bx[0:HH, k:k + N], w_t[par][:, t, q], xt[:, :], start=True, stop=True)
                ins.then_inc(t_psum, 1)

            def project_pq(n, par):
                nc.tensor.matmul(bx[:, 0:2 * H], xt[:, :], w_nat[par][:, :, :].rearrange("p t h -> p (t h)"),
                                 start=True, stop=True).then_inc(pq_psum, 1)

            def transpose_hm(o):
                pe.wait_ge(hm_ready, o + 1)
                for t in range(2):
                    ins = nc.tensor.transpose(by[0:HH, N * t:N * t + N], hm[:, t], ident[:, :])
                ins.then_inc(hmt_psum, 1)

            def layer0(o, par):
                pe.wait_ge(hmt_copied, o + 1)
                for t in range(2):
                    nc.tensor.matmul(bx[:, 0:F], hm_t[:, t], w2_sb[:, t], start=(t == 0), stop=False)
                for i in range(PARTS):
                    ins = nc.tensor.matmul(bx[:, 0:F], mask[par][:, :], hi(b2_parts[:, i])[:, 1::2],
                                           start=False, stop=(i == PARTS - 1))
                ins.then_inc(l0_psum, 1)

            def transpose_x1(pair):
                pe.wait_ge(x1_ready, 2 * pair + 2)
                nc.tensor.transpose(by[:, 0:N], x1[:, :, :].rearrange("p b f -> p (b f)"), ident[:, :])\
                    .then_inc(x1t_psum, 1)

            def contract(u, par):
                ring = ind_v if u % 2 else ind_a
                half, col = divmod(HU * u, HH)
                sums_out = s_bank[half][:, 0:(PARTS + 1) * HH].rearrange("p (i h) -> p i h", i=PARTS + 1)
                qv = hi(qn[par][:, :, :].rearrange("p i h -> p (i h)")).rearrange(
                    "p (i h e) -> p i h e", i=PARTS + 1, e=2)
                for h in range(HU):
                    ins = nc.tensor.matmul(sums_out[:, :, col + h],
                                           ring[(u // 2) % RING][:, N * h:N * h + N],
                                           qv[:, :, HU * u + h, 1], start=True, stop=True)
                ins.then_inc(contracted, 1)

            def difference(u, par):
                c, s = divmod(u, SETS)
                c1, q = divmod(c, HQ)
                bank = d_bank[u % BANKS]
                if u in (0, 2):
                    nc.tensor.matmul(bank[:, :].rearrange("p (h k) -> p h k", k=N), neg_big[:, :],
                                     nmask[par][:, :].unsqueeze(1).broadcast_to([128, HU, N]),
                                     start=True, stop=True, skip_group_check=True)
                wv = hi(wq[par][:, c1, s, q])[:, 1::2]
                m = hi(mv[par][:, :, :, :, :].rearrange("p h c q k -> p (h c q k)")).rearrange(
                    "p (h c q k e) -> p h c q k e", h=HU, c=C1, q=HQ, e=2)[:, :, c1, q, :, 1]
                nc.tensor.matmul(bank[:, :].rearrange("p (h k) -> p h k", k=N), wv, m, start=bool(u % 2), stop=True,
                                 skip_group_check=True)\
                    .then_inc(d_for_dve if u % 2 else d_for_act, 1)

            pe.wait_ge(weights_ready, 2)
            nc.tensor.matmul(by[:, 0:H], ones[:, :], b1_row[:, :], start=True, stop=True)
            nc.tensor.matmul(by[:, H:H + F], ones[:, :], b2_row[:, :], start=True, stop=True)
            for q in range(HQ):
                ins = nc.tensor.matmul(bx[0:HH, q:q + 1], b1_t[:, q], ones[:, 0:1], start=True, stop=True)
            ins.then_inc(bias_psum, 1)
            pe.wait_ge(bias_ready, 1)
            transpose_xt(0)
            pe.wait_ge(xt_copied, 1)
            project_t(0, 0)
            transpose_at(0, 0)
            pe.wait_ge(t_copied, 2)
            project_pq(0, 0)
            pe.wait_ge(qn_ones, 2)
            pe.wait_ge(w2_in, 16)

            def graph(b, par, first, last, last_pair=False):
                for u in range(UNITS):
                    if u == 0 and not last:
                        pe.wait_ge(pq_copied, b + 1)
                        if par == 1:
                            pe.wait_ge(xt_copied, b // 2 + 2)
                        project_t(b + 1, 1 - par)
                    if u == 6 and not last:
                        if par == 1:
                            pe.wait_ge(xt_copied, b // 2 + 2)
                            if not (isinstance(b, int) and b == 1):
                                pe.wait_ge(x1t_copied, b // 2)
                        elif first:
                            pe.wait_ge(at_copied, 1)
                        else:
                            pe.wait_ge(hmt_copied, b - 1)
                        transpose_at(b + 1, 1 - par)
                    if u == 22 and not first:
                        if last:
                            pe.wait_ge(x1t_copied, b // 2)
                        else:
                            pe.wait_ge(at_copied, b + 2)
                        transpose_hm(b - 1)
                    if u == 28 and not first:
                        if last:
                            pe.wait_ge(pq_copied, b + 1)
                        else:
                            pe.wait_ge(t_copied, 2 * b + 4)
                        layer0(b - 1, 1 - par)
                    if u == 34 and not last:
                        if first:
                            pe.wait_ge(t_copied, 2 * b + 4)
                        else:
                            pe.wait_ge(l0_added, b)
                        project_pq(b + 1, 1 - par)
                    if u == 38 and par == 0 and not last_pair:
                        if first:
                            pe.wait_ge(at_copied, b + 2)
                        else:
                            pe.wait_ge(hmt_copied, b)
                        transpose_xt(b // 2 + 1)
                    if u == 45 and par == 0 and not first:
                        if last_pair:
                            pe.wait_ge(hmt_copied, b)
                        else:
                            pe.wait_ge(xt_copied, b // 2 + 2)
                        transpose_x1(b // 2 - 1)
                    if u == 0:
                        pe.wait_ge(wq_loaded, 16 * WLOADS * (b + 1))
                        pe.wait_ge(mv_loaded, 16 * (b + 1))
                        pe.wait_ge(masks_made, b + 1)
                    if not (first and u < BANKS):
                        pe.wait_ge(dve_ind if u % 2 else act_ind, EU * b + u // 2 - 1)
                    difference(u, par)
                    if u == LAG:
                        pe.wait_ge(q_split, b + 1)
                        if not first:
                            pe.wait_ge(s_copied, 2 * b - 1)
                    if u == LAG + HALF_UNITS and not first:
                        pe.wait_ge(s_copied, 2 * b)
                    if u >= LAG:
                        contract(u - LAG, par)
                    elif not first:
                        contract(UNITS + u - LAG, 1 - par)

            graphs(pe, graph)
            pe.wait_ge(act_ind, EU * NB)
            pe.wait_ge(dve_ind, EU * NB)
            for u in range(UNITS - LAG, UNITS):
                contract(u, 1)
            pe.wait_ge(hmt_copied, NB - 1)
            transpose_hm(NB - 1)
            pe.wait_ge(l0_added, NB - 1)
            layer0(NB - 1, 1)
            transpose_x1(PAIRS - 1)

            pe.wait_ge(bn_ready, 1)
            nc.tensor.matmul(bx[:, 0:2], havg[:, :], bn_mv[:, :], start=True, stop=True)
            nc.tensor.matmul(bx[:, 2:3], hdif[:, :], bn_mv[:, 0:1], start=True, stop=True).then_inc(bn_comb, 1)

            def project_x(g):
                if g >= 4:
                    pe.wait_ge(xe_ready, g - 3)
                for k in range(GB // 2):
                    nc.tensor.matmul(x_bank[g % 4][:, 2 * F * k:2 * F * k + 2 * F],
                                     x1t_all[:, GB // 2 * g + k], w_bn[:, :, :].rearrange("p a f -> p (a f)"),
                                     start=(k == 0), stop=False, skip_group_check=True)

            def add_e(g):
                nc.tensor.matmul(x_bank[g % 4][:, :].rearrange("p (b f) -> p b f", f=F), ones_bf[:, :],
                                 hi(e_sel[:, :])[:, 1::2].unsqueeze(1).broadcast_to([PARTS, GB, F]),
                                 start=False, stop=True, skip_group_check=True).then_inc(xw_psum, 1)

            pe.wait_ge(wbn_ready, 1)
            for g in range(2):
                project_x(g)
            pe.wait_ge(shift_ready, 1)
            nc.tensor.matmul(by[0:PARTS, 0:F], shift[:, :], lw[0:F], start=True, stop=False)
            nc.tensor.matmul(by[0:PARTS, 0:F], ones[:, 0:PARTS], lb_row[:, :], start=False, stop=True)\
                .then_inc(e_psum, 1)
            for g in range(2, 4):
                project_x(g)
            pe.wait_ge(e_ready, 1)
            for g in range(4):
                add_e(g)
            for g in range(GROUPS):
                if g == 0:
                    pe.wait_ge(at_scaled, NB)
                pe.wait_ge(xe_ready, g + 1)
                if g >= 4:
                    pe.wait_ge(zz_ready, g - 3)
                for k in range(GB):
                    ins = nc.tensor.matmul(a_bank[g % 4][:, F * k:F * k + F], at_all[:, GB * g + k],
                                           xe[g][:, k], start=True, stop=True)
                ins.then_inc(ax_psum, 1)
                if g + 4 < GROUPS:
                    project_x(g + 4)
                    add_e(g + 4)


_INS = ["x", "adj", "L0_gnn_W1", "L0_gnn_b1", "L0_gnn_W2", "L0_gnn_b2",
        "L1_gnn_gamma", "L1_gnn_beta", "L1_gnn_W", "L1_gnn_b"]
_OUTS = [((64, 128, 64), "float32")]


def kernel(**inputs):
    import numpy as _np
    import concourse.bacc as _bacc
    from concourse import mybir as _mybir
    from concourse.bass_utils import run_bass_kernel_spmd as _run

    nc = _bacc.Bacc("TRN2", target_bir_lowering=False, num_devices=1)
    arrays, args = {}, []
    for name in _INS:
        a = _np.ascontiguousarray(inputs[name])
        arrays[f"in_{name}_dram"] = a
        args.append(nc.dram_tensor(f"in_{name}_dram", a.shape, _mybir.dt.from_np(a.dtype), kind="ExternalInput").ap())
    for i, (shape, dtype) in enumerate(_OUTS):
        dt = _mybir.dt.from_np(_np.dtype(dtype))
        args.append(nc.dram_tensor(f"out_{i}_dram", shape, dt, kind="ExternalOutput").ap())
    gnn_kernel(nc, *args)
    r = _run(nc, [arrays], core_ids=[0])
    return r.results[0]["out_0_dram"]
```

```python
import concourse.bass as bass
from concourse import mybir
from contextlib import ExitStack


def gnn_kernel(nc, x, adj, W1, b1, W2, b2, gamma, beta, W, bvec, out):
    f32, bf16 = mybir.dt.float32, mybir.dt.bfloat16
    ALU, ACT, AX = mybir.AluOpType, mybir.ActivationFunctionType, mybir.AxisListType

    NB, N, F = x.shape
    H = W1.shape[1]
    EPS = 1e-5
    HU = 4
    UNITS = H // HU
    SETS = 8
    C1, HQ = 3, 2
    HH = H // 2
    HALF_UNITS = UNITS // 2
    PARTS = 3
    PROWS, QROWS = PARTS, PARTS * HU
    QP0 = PROWS * SETS
    BANKS = 4
    LAG = 4
    RING = 4
    BIG = float(2 ** 60)
    PAIRS = NB // 2
    EU = UNITS // 2
    WLOADS, QSTORES = SETS, C1
    assert UNITS == SETS * C1 * HQ and N == 128 and 2 * F == 128

    ctx = ExitStack()
    with ctx:
        def sb(name, shape, dt=f32):
            return ctx.enter_context(nc.sbuf_tensor(name, shape, dt))

        def sem(name):
            return ctx.enter_context(nc.semaphore(name))

        GB = 8
        GROUPS = NB // GB

        wq = [sb(f"wq{i}", [128, C1, SETS, HQ, N]) for i in range(2)]
        mv = [sb(f"mv{i}", [128, HU, C1, HQ, N]) for i in range(2)]
        tparts = [sb(f"tparts{i}", [HH, PARTS, 2, HQ, N]) for i in range(2)]
        at_all = sb("at_all", [128, NB, N])
        at_raw = sb("at_raw", [128, N])
        at_less = sb("at_less", [128, N])
        x_all = sb("x_all", [128, NB, F])
        x1t_all = sb("x1t_all", [128, PAIRS, N])
        a_in = [sb(f"a_in{i}", [128, N]) for i in range(2)]
        x_in = sb("x_in", [128, 2, F])
        xt = sb("xt", [128, N])
        qn = [sb(f"qn{i}", [128, PARTS + 1, H]) for i in range(2)]
        pn = [sb(f"pn{i}", [128, H]) for i in range(2)]
        ind_a = [sb(f"ind_a{i}", [128, HU * N], bf16) for i in range(RING)]
        ind_v = [sb(f"ind_v{i}", [128, HU * N], bf16) for i in range(RING)]
        mask = [sb(f"mask{i}", [128, N], bf16) for i in range(2)]
        nmask = [sb(f"nmask{i}", [128, N], bf16) for i in range(2)]
        sums = [sb(f"sums{i}", [128, 2, PARTS + 1, HH]) for i in range(2)]
        hm = sb("hm", [128, 2, HH])
        hm_t = sb("hm_t", [HH, 2, N])
        d_now = [sb(f"d_now{i}", [128, 1]) for i in range(2)]
        rs_now = [sb(f"rs_now{i}", [128, 1]) for i in range(2)]
        x1 = sb("x1", [128, 2, F])
        ln_stats = sb("ln_stats", [128, 6])
        ln_mv = sb("ln_mv", [128, 2])
        ln_var = sb("ln_var", [128, 1])
        ln_rstd = sb("ln_rstd", [128, 1])
        ones_n = sb("ones_n", [128, N], bf16)
        eps = sb("eps", [128, GB])
        half_down = sb("half_down", [128, GB])
        ident = sb("ident", [128, 128])
        neg_big = sb("neg_big", [128, 128], bf16)
        pat_w = sb("pat_w", [128, SETS])
        pat_m = sb("pat_m", [128, HU])
        ones = sb("ones", [1, 128])
        w_raw = sb("w_raw", [128, 2, H])
        w_sign = sb("w_sign", [128, 2, H])
        w_diff = sb("w_diff", [128, 2, H])
        w_nat = [sb(f"w_nat{i}", [128, 2, H]) for i in range(2)]
        w_t = [sb(f"w_t{i}", [128, 2, HQ, HH]) for i in range(2)]
        b1_row = sb("b1_row", [1, H])
        b1_diff = sb("b1_diff", [1, H])
        b1_t = sb("b1_t", [1, HQ, HH])
        b2_row = sb("b2_row", [1, F])
        b1_all = sb("b1_all", [128, H])
        b1t_all = sb("b1t_all", [HH, HQ])
        b2_parts = sb("b2_parts", [128, PARTS, F])
        w2_sb = sb("w2_sb", [HH, 2, F])
        lw = sb("lw", [128, F])
        lb_row = sb("lb_row", [1, F])
        gb = sb("gb", [128, 2])
        havg = sb("havg", [128, 128])
        hdif = sb("hdif", [128, 128])
        bn_st = sb("bn_st", [128, 8, 6])
        bn_mv = sb("bn_mv", [128, 2])
        bn = sb("bn", [128, 8])
        w_bn = sb("w_bn", [128, 2, F])
        shift = sb("shift", [F, PARTS])
        e_parts = sb("e_parts", [PARTS, PARTS, F])
        e_sel = sb("e_sel", [PARTS, F])
        ones_bf = sb("ones_bf", [PARTS, N], bf16)
        nsd_all = sb("nsd_all", [128, NB])
        l1_tiles = [t[:, :, :, :, :].rearrange("p c s q k -> p (c s q k)").rearrange(
            "p (t b f) -> p t b f", b=GB, f=F) for t in wq]
        xe, zz = ([l1_tiles[i][:, g] for g in range(GROUPS)] for i in range(2))
        g_st = [sb(f"g_st{i}", [128, GB, 6]) for i in range(2)]
        g_mv = [sb(f"g_mv{i}", [128, GB, 2]) for i in range(2)]
        g_scale = [sb(f"g_scale{i}", [128, GB]) for i in range(2)]
        g_shift = [sb(f"g_shift{i}", [128, GB]) for i in range(2)]

        d_bank = [ctx.enter_context(nc.psum_tensor(f"d_bank{i}", [128, 512], f32)) for i in range(BANKS)]
        s_bank = [ctx.enter_context(nc.psum_tensor(f"s_bank{i}", [128, 512], f32)) for i in range(2)]
        bx = ctx.enter_context(nc.psum_tensor("bx", [128, 512], f32))
        by = ctx.enter_context(nc.psum_tensor("by", [128, 512], f32))

        x_bank = [d_bank[0], d_bank[1], s_bank[0], s_bank[1]]
        a_bank = [d_bank[2], d_bank[3], bx, by]

        q_dram = [nc.dram_tensor(f"q_scratch{i}", (SETS, HU, PARTS, C1, HQ * N), f32, kind="Internal").ap()
                  for i in range(2)]
        p_dram = [nc.dram_tensor(f"p_scratch{i}", (PARTS, HH, HQ * N), f32, kind="Internal").ap()
                  for i in range(2)]

        w1_in, w2_in, b_in, l1_in, x_all_in = (sem(n) for n in ("w1_in", "w2_in", "b_in", "l1_in", "x_all_in"))
        a_loaded, x_loaded = [sem(f"a_loaded{i}") for i in range(2)], sem("x_loaded")
        pool_step, dve_step = sem("pool_step"), sem("dve_step")
        pats_ready, ident_ready, weights_ready = sem("pats_ready"), sem("ident_ready"), sem("weights_ready")
        bias_psum, bias_ready, qn_ones = sem("bias_psum"), sem("bias_ready"), sem("qn_ones")
        bias_t_psum, bias_t_ready, w_t_ready = sem("bias_t_psum"), sem("bias_t_ready"), sem("w_t_ready")
        wq_init = [sem(f"wq_init{i}") for i in range(2)]
        mv_init = [sem(f"mv_init{i}") for i in range(2)]
        xt_psum, xt_copied = sem("xt_psum"), sem("xt_copied")
        at_psum, at_copied = sem("at_psum"), sem("at_copied")
        t_psum, t_copied, tq_split, tp_split = (sem(n) for n in ("t_psum", "t_copied", "tq_split", "tp_split"))
        pq_psum, pq_copied, q_split = sem("pq_psum"), sem("pq_copied"), sem("q_split")
        q_stored, p_stored = sem("q_stored"), sem("p_stored")
        wq_loaded, mv_loaded = sem("wq_loaded"), sem("mv_loaded")
        d_done, masks_made = sem("d_done"), sem("masks_made")
        d_for_act, d_for_dve = sem("d_for_act"), sem("d_for_dve")
        act_ind, dve_ind, contracted = sem("act_ind"), sem("dve_ind"), sem("contracted")
        s_copied, hm_step, hm_ready = sem("s_copied"), sem("hm_step"), sem("hm_ready")
        hmt_psum, hmt_copied, l0_psum, l0_added = (sem(n) for n in ("hmt_psum", "hmt_copied", "l0_psum", "l0_added"))
        ln_step, x1_ready, x1_kept = sem("ln_step"), sem("x1_ready"), sem("x1_kept")
        x1t_psum, x1t_copied = sem("x1t_psum"), sem("x1t_copied")
        t_step, q_step, pow_consts = sem("t_step"), sem("q_step"), sem("pow_consts")
        var_ready, rstd_step, rstd_ready = sem("var_ready"), sem("rstd_step"), sem("rstd_ready")
        bn_var, bn_rstd = sem("bn_var"), sem("bn_rstd")
        stats_made, bn_ready, bn_comb, wbn_ready, e_psum = sem("stats_made"), sem("bn_ready"), sem("bn_comb"), sem("wbn_ready"), sem("e_psum")
        shift_ready, e_ready = sem("shift_ready"), sem("e_ready")
        rs_ready, less_ready, at_scaled = sem("rs_ready"), sem("less_ready"), sem("at_scaled")
        nmask_made, ones_made, centred = sem("nmask_made"), sem("ones_made"), sem("centred")
        nsd_made = sem("nsd_made")
        xw_psum, xe_ready, ax_psum = sem("xw_psum"), sem("xe_ready"), sem("ax_psum")
        zz_ready, zl_ready = sem("zz_ready"), sem("zl_ready")
        y2_ready, g_mv_ready = sem("y2_ready"), sem("g_mv_ready")
        g_step, g_ready, yf_ready = sem("g_step"), sem("g_ready"), sem("yf_ready")
        last_ready = sem("last_ready")
        out_stored = sem("out_stored")

        block = ctx.enter_context(nc.Block())

        def hi(ap):
            return ap.bitcast(bf16)

        def graphs(eng, program):
            program(0, 0, True, False)
            program(1, 1, False, False)
            with eng.Fori(1, PAIRS - 1) as pair:
                program(2 * pair, 0, False, False)
                program(2 * pair + 1, 1, False, False)
            program(NB - 2, 0, False, False, True)
            program(NB - 1, 1, False, True, True)

        @block.sync
        def _(sp):
            sp.dma_start(x_in[:, :, :], x[0:2].rearrange("b j f -> j b f")).then_inc(x_loaded, 16)
            w1_v = W1.rearrange("(t f) h -> f t h", t=2)
            sp.dma_start(w_raw[0:F], w1_v).then_inc(w1_in, 16)
            sp.dma_start(w_raw[F:128], w1_v).then_inc(w1_in, 16)
            sp.dma_start(b1_row[:, :], b1.rearrange("(a h) -> a h", a=1)).then_inc(b_in, 16)
            sp.dma_start(a_in[0][:, :], adj[0]).then_inc(a_loaded[0], 16)
            sp.dma_start(b2_row[:, :], b2.rearrange("(a h) -> a h", a=1)).then_inc(b_in, 16)
            sp.dma_start(a_in[1][:, :], adj[1]).then_inc(a_loaded[1], 16)
            sp.dma_start(w2_sb[:, :, :], W2.rearrange("(t h) o -> h t o", t=2)).then_inc(w2_in, 16)

            def value(v):
                if isinstance(v, int):
                    return v
                reg = sp.alloc_register()
                sp.reg_mov(reg, v)
                return sp.snap(reg, donate=True)

            def counts(n):
                return {"parts": value(n + 1), "wq_before": value(16 * WLOADS * (n - 1)),
                        "mv_before": value(16 * (n - 1)), "d_before": value(EU * (n - 1)),
                        "q_stored": value(16 * QSTORES * (n + 1)), "p_stored": value(16 * (n + 1))}

            def operands(cnt, par, first_use):
                sp.wait_ge(tq_split, cnt["parts"])
                if not first_use:
                    sp.wait_ge(wq_loaded, cnt["wq_before"])
                    sp.wait_ge(mv_loaded, cnt["mv_before"])
                for c1 in range(C1):
                    sp.dma_start(q_dram[par][:, :, :, c1].rearrange("s h i k -> (s h) i k"),
                                 tparts[par][c1:HH:C1, :, 1].rearrange("p i q k -> p i (q k)")).then_inc(q_stored, 16)
                sp.wait_ge(tp_split, cnt["parts"])
                sp.dma_start(p_dram[par].rearrange("i t k -> t i k"),
                             tparts[par][:, :, 0].rearrange("p i q k -> p i (q k)")).then_inc(p_stored, 16)
                if first_use:
                    sp.wait_ge(wq_init[par], C1)
                    sp.wait_ge(mv_init[par], 1)
                else:
                    sp.wait_ge(d_for_dve, cnt["d_before"])
                sp.wait_ge(q_stored, cnt["q_stored"])
                for s in range(SETS):
                    sp.dma_start(wq[par][QP0 + s:QP0 + SETS * QROWS:SETS, :, s].rearrange("r c q k -> r c (q k)"),
                                 q_dram[par][s].rearrange("h i c k -> (h i) c k")).then_inc(wq_loaded, 16)
                sp.wait_ge(p_stored, cnt["p_stored"])
                sp.dma_start(mv[par][0:QP0].rearrange("p h c q k -> p (h c q k)"),
                             p_dram[par].rearrange("i (s m) k -> (i s) (m k)", s=SETS)).then_inc(mv_loaded, 16)

            operands(counts(0), 0, True)
            def graph(b, par, first, last, last_pair=False):
                ahead, done, pairs_done = value(b + 2), value(b + 1), value(b // 2 + 1)
                cnt = counts(b + 1)
                if not last_pair:
                    sp.wait_ge(at_psum, done)
                    sp.wait_ge(d_done, done)
                    sp.dma_start(a_in[par][:, :], adj[bass.ds(ahead, 1)].rearrange("a j k -> (a j) k"))\
                        .then_inc(a_loaded[par], 16)
                if par == 0 and not last_pair:
                    sp.wait_ge(xt_psum, pairs_done)
                    sp.dma_start(x_in[:, :, :], x[bass.ds(ahead, 2)].rearrange("b j f -> j b f"))\
                        .then_inc(x_loaded, 16)
                if not last:
                    operands(cnt, 1 - par, first)
                if first:
                    sp.dma_start(x_all[:, :, :], x.rearrange("b j f -> j b f")).then_inc(x_all_in, 16)
                    for i in range(2):
                        rows = slice(F * i, F * i + F)
                        sp.dma_start(lw[rows], W).then_inc(l1_in, 16)
                        sp.dma_start(gb[rows, 0:1], gamma.rearrange("(c a) -> c a", a=1)).then_inc(l1_in, 16)
                        sp.dma_start(gb[rows, 1:2], beta.rearrange("(c a) -> c a", a=1)).then_inc(l1_in, 16)
                    sp.dma_start(lb_row[:, :], bvec.rearrange("(a h) -> a h", a=1)).then_inc(l1_in, 16)

            graphs(sp, graph)

            for g in range(GROUPS):
                sp.wait_ge(yf_ready, g + 1)
                if g == GROUPS - 1:
                    sp.wait_ge(last_ready, 1)
                sp.dma_start(out[GB * g:GB * g + GB].rearrange("b j o -> j b o"), x_all[:, GB * g:GB * g + GB])\
                    .then_inc(out_stored, 16)
            sp.wait_ge(out_stored, 16 * GROUPS)

        @block.gpsimd
        def _(pool):
            steps = [0]

            def link(ins):
                steps[0] += 1
                ins.then_inc(pool_step, 1)
                pool.wait_ge(pool_step, steps[0])

            link(nc.gpsimd.memset(ident[:, :], 0.0))
            nc.gpsimd.affine_select(out=ident[:, :], in_=ident[:, :], compare_op=ALU.not_equal, fill=1.0,
                                    base=0, pattern=[[-1, 128]], channel_multiplier=1).then_inc(ident_ready, 1)
            link(nc.gpsimd.memset(pat_w[:, :], 0.0))
            for i in range(PROWS):
                link(nc.gpsimd.affine_select(out=pat_w[:, :], in_=pat_w[:, :], compare_op=ALU.not_equal, fill=1.0,
                                             base=-SETS * i, pattern=[[-1, SETS]], channel_multiplier=1))
            rows = SETS * PARTS
            link(nc.gpsimd.memset(pat_m[:, :], 1.0))
            link(nc.gpsimd.affine_select(out=pat_m[:, :], in_=pat_m[:, :], compare_op=ALU.is_ge, fill=0.0,
                                         base=-QP0, pattern=[[-rows, HU]], channel_multiplier=1))
            nc.gpsimd.affine_select(out=pat_m[:, :], in_=pat_m[:, :], compare_op=ALU.is_ge, fill=0.0,
                                    base=QP0 + rows - 1, pattern=[[rows, HU]], channel_multiplier=-1)\
                .then_inc(pats_ready, 1)
            nc.gpsimd.memset(ones_n[:, :], 1.0).then_inc(ones_made, 1)
            for i in range(2):
                nc.gpsimd.memset(qn[i][:, PARTS], 1.0).then_inc(qn_ones, 1)
            nc.gpsimd.memset(eps[:, :], EPS).then_inc(pow_consts, 1)
            nc.gpsimd.memset(half_down[:, :], -0.5).then_inc(pow_consts, 1)

            def split_t(n, par):
                for t in (1, 0):
                    pool.wait_ge(t_copied, 2 * n + 2 - t)
                    for i in range(1, PARTS):
                        part = tparts[par][:, i, t].rearrange("p q k -> p (q k)")
                        before = tparts[par][:, i - 1, t].rearrange("p q k -> p (q k)")
                        if i == 2:
                            pool.wait_ge(t_step, 2 * n + (1 if t else 2))
                        nc.gpsimd.tensor_tensor(part, before, hi(before)[:, 1::2], ALU.subtract)\
                            .then_inc(t_step if i == 1 else tq_split if t else tp_split, 1)

            def split_q(n, par):
                pool.wait_ge(pq_copied, n + 1)
                nc.gpsimd.tensor_tensor(pn[par][:, :], pn[par][:, :], b1_all[:, :], ALU.add).then_inc(q_step, 1)
                for i in range(1, PARTS):
                    t = qn[par]
                    if i == 2:
                        pool.wait_ge(q_step, 2 * n + 2)
                    nc.gpsimd.tensor_tensor(t[:, i], t[:, i - 1], hi(t[:, i - 1])[:, 1::2], ALU.subtract)\
                        .then_inc(q_step if i == 1 else q_split, 1)

            def degree_power(n, par):
                pool.wait_ge(d_done, n + 1)
                nc.gpsimd.tensor_tensor(rs_now[par][:, :], d_now[par][:, :], half_down[:, 0:1], ALU.pow)\
                    .then_inc(rs_ready, 1)

            def subtract_identity(n):
                pool.wait_ge(at_copied, n + 1)
                if not (isinstance(n, int) and n == 0):
                    pool.wait_ge(at_scaled, n)
                nc.gpsimd.tensor_tensor(at_less[:, :], at_raw[:, :], ident[:, :], ALU.subtract)\
                    .then_inc(less_ready, 1)

            def complement(n, par):
                pool.wait_ge(masks_made, n + 1)
                nc.gpsimd.tensor_tensor(nmask[par][:, :], ones_n[:, :], mask[par][:, :], ALU.subtract)\
                    .then_inc(nmask_made, 1)

            def finish_hm(o, par, first):
                pool.wait_ge(s_copied, 2 * o + 2)
                if not first:
                    pool.wait_ge(hmt_psum, o)
                nc.gpsimd.tensor_tensor(hm[:, :, :], pn[par][:, :].rearrange("p (t h) -> p t h", t=2),
                                        sums[par][:, :, PARTS], ALU.mult).then_inc(hm_step, 1)
                for i in range(PARTS):
                    pool.wait_ge(hm_step, PARTS * o + i + 1)
                    nc.gpsimd.tensor_tensor(hm[:, :, :], hm[:, :, :], sums[par][:, :, i], ALU.subtract)\
                        .then_inc(hm_ready if i == PARTS - 1 else hm_step, 1)

            def apply_norm(o, par):
                nc.gpsimd.tensor_tensor(x1[:, par], x1[:, par], ln_mv[:, 0:1].broadcast_to([128, F]), ALU.subtract)\
                    .then_inc(centred, 1)
                pool.wait_ge(centred, o + 1)
                pool.wait_ge(rstd_ready, o + 1)
                nc.gpsimd.tensor_tensor(x1[:, par], x1[:, par], ln_rstd[:, 0:1].broadcast_to([128, F]), ALU.mult)\
                    .then_inc(x1_ready, 1)

            def rstd(o):
                pool.wait_ge(var_ready, o + 1)
                nc.gpsimd.tensor_tensor(ln_var[:, :], ln_mv[:, 1:2], eps[:, 0:1], ALU.add).then_inc(rstd_step, 1)
                pool.wait_ge(rstd_step, o + 1)
                nc.gpsimd.tensor_tensor(ln_rstd[:, :], ln_var[:, :], half_down[:, 0:1], ALU.pow)\
                    .then_inc(rstd_ready, 1)

            split_t(0, 0)
            pool.wait_ge(pow_consts, 2)
            degree_power(0, 0)
            pool.wait_ge(ones_made, 1)
            complement(0, 0)
            subtract_identity(0)
            pool.wait_ge(bias_ready, 1)
            split_q(0, 0)

            def graph(b, par, first, last, last_pair=False):
                if not last:
                    split_t(b + 1, 1 - par)
                    degree_power(b + 1, 1 - par)
                if not first:
                    finish_hm(b - 1, 1 - par, isinstance(b, int) and b == 1)
                if not last:
                    subtract_identity(b + 1)
                if not first:
                    rstd(b - 1)
                    apply_norm(b - 1, 1 - par)
                if not last:
                    complement(b + 1, 1 - par)
                    split_q(b + 1, 1 - par)
                if par == 0 and not first:
                    keep_x1(b)

            def keep_x1(b):
                pool.wait_ge(x1_ready, b)
                nc.gpsimd.tensor_copy(x_all[:, bass.ds(b - 2, 2)], x1[:, :, :]).then_inc(x1_kept, 1)

            graphs(pool, graph)
            rstd(NB - 1)
            apply_norm(NB - 1, 1)
            keep_x1(NB)

            pool.wait_ge(bn_var, 1)
            nc.gpsimd.tensor_tensor(bn[:, 4:5], bn[:, 3:4], half_down[:, 0:1], ALU.pow).then_inc(bn_rstd, 1)

            def add_x(g):
                pool.wait_ge(zl_ready, g + 1)
                if g == 0:
                    pool.wait_ge(x1_kept, PAIRS)
                nc.gpsimd.tensor_tensor(x_all[:, GB * g:GB * g + GB], zz[g], x_all[:, GB * g:GB * g + GB], ALU.add)\
                    .then_inc(y2_ready, 1)

            def scale_shift(g):
                i = g % 2
                pool.wait_ge(g_mv_ready, g + 1)
                if g >= 2:
                    pool.wait_ge(yf_ready, g - 1)
                nc.gpsimd.tensor_tensor(g_scale[i][:, :], g_mv[i][:, :, 1], half_down[:, 0:GB], ALU.pow)\
                    .then_inc(g_step, 1)
                pool.wait_ge(g_step, g + 1)
                nc.gpsimd.tensor_tensor(g_shift[i][:, :], g_mv[i][:, :, 0], g_scale[i][:, :], ALU.mult)\
                    .then_inc(g_ready, 1)

            for g in range(GROUPS + 1):
                if g < GROUPS:
                    add_x(g)
                if g >= 1:
                    scale_shift(g - 1)

        @block.scalar
        def _(act):
            def fill_mv(i):
                nc.scalar.activation(mv[i][:, :, :, :, :].rearrange("p h c q k -> p h (c q k)"),
                                     pat_m[:, :].unsqueeze(2).broadcast_to([128, HU, C1 * HQ * N]), ACT.Copy)\
                    .then_inc(mv_init[i], 1)

            def fill_wq(i, c):
                nc.scalar.activation(wq[i][:, c].rearrange("p s q k -> p s (q k)"),
                                     pat_w[:, :].unsqueeze(2).broadcast_to([128, SETS, HQ * N]), ACT.Copy)\
                    .then_inc(wq_init[i], 1)

            def copy_xt(pair):
                act.wait_ge(xt_psum, pair + 1)
                nc.scalar.activation(xt[:, :], by[:, 0:N], ACT.Copy).then_inc(xt_copied, 1)

            def copy_t_q(n, par, first_use):
                act.wait_ge(t_psum, n + 1)
                if not first_use:
                    act.wait_ge(q_stored, 16 * QSTORES * (n - 1))
                    act.wait_ge(p_stored, 16 * (n - 1))
                nc.scalar.activation(tparts[par][:, 0, 1].rearrange("p q k -> p (q k)"),
                                     bx[0:HH, HQ * N:2 * HQ * N], ACT.Copy).then_inc(t_copied, 1)

            def copy_t_p(par):
                for q in range(HQ):
                    ins = nc.scalar.activation(tparts[par][:, 0, 0, q], bx[0:HH, N * q:N * q + N], ACT.Identity,
                                               bias=b1t_all[:, q:q + 1])
                ins.then_inc(t_copied, 1)

            def copy_at(n, first_use):
                act.wait_ge(at_psum, n + 1)
                if not first_use:
                    act.wait_ge(masks_made, n)
                    act.wait_ge(less_ready, n)
                nc.scalar.activation(at_raw[:, :], by[:, 0:N], ACT.Copy).then_inc(at_copied, 1)

            def scale_at(n, par):
                act.wait_ge(less_ready, n + 1)
                act.wait_ge(rs_ready, n + 1)
                nc.scalar.activation(at_all[:, bass.ds(n, 1)].rearrange("p a k -> p (a k)"), at_less[:, :],
                                     ACT.Identity, scale=rs_now[par][:, 0:1]).then_inc(at_scaled, 1)

            def copy_p(n, par, first_use):
                act.wait_ge(pq_psum, n + 1)
                if not first_use:
                    act.wait_ge(contracted, UNITS * (n - 1))
                    act.wait_ge(hm_ready, n - 1)
                nc.scalar.activation(pn[par][:, :], bx[:, 0:H], ACT.Copy)

            def copy_q(par):
                nc.scalar.activation(qn[par][:, 0], bx[:, H:2 * H], ACT.Copy).then_inc(pq_copied, 1)

            def copy_sums(b, par, half, first_use):
                act.wait_ge(contracted, UNITS * b + HALF_UNITS * (half + 1))
                if not first_use and half == 0:
                    act.wait_ge(hm_ready, b - 1)
                nc.scalar.activation(sums[par][:, half].rearrange("p i h -> p (i h)"),
                                     s_bank[half][:, 0:(PARTS + 1) * HH], ACT.Copy).then_inc(s_copied, 1)

            def copy_hmt(o, first_use):
                act.wait_ge(hmt_psum, o + 1)
                if not first_use:
                    act.wait_ge(l0_psum, o)
                nc.scalar.activation(hm_t[:, :, :].rearrange("p t k -> p (t k)"), by[0:HH, 0:2 * N], ACT.Copy)\
                    .then_inc(hmt_copied, 1)

            def copy_x1t(pair):
                act.wait_ge(x1t_psum, pair + 1)
                nc.scalar.activation(x1t_all[:, bass.ds(pair, 1)].rearrange("p a k -> p (a k)"), by[:, 0:N], ACT.Copy)\
                    .then_inc(x1t_copied, 1)

            act.wait_ge(pats_ready, 1)
            fill_mv(0)
            copy_xt(0)
            copy_at(0, True)
            fill_wq(0, 1)
            act.wait_ge(bias_t_ready, 1)
            copy_t_q(0, 0, True)
            copy_t_p(0)
            copy_p(0, 0, True)
            copy_q(0)
            fill_wq(0, 2)
            fill_mv(1)
            fill_wq(1, 2)
            nc.scalar.preload_act_table(ACT.Sigmoid)

            def graph(b, par, first, last, last_pair=False):
                for v in range(EU):
                    act.wait_ge(d_for_act, EU * b + v + 1)
                    if not (first and v < RING):
                        act.wait_ge(contracted, UNITS * b + 2 * (v - RING) + 1)
                    nc.scalar.activation(ind_a[v % RING][:, :], d_bank[2 * v % BANKS][:, :], ACT.Sigmoid, scale=BIG)\
                        .then_inc(act_ind, 1)
                    if v == 0 and not last:
                        copy_t_q(b + 1, 1 - par, first)
                    if v == 1 and not last:
                        copy_t_p(1 - par)
                    if v == 3 and not first:
                        copy_sums(b - 1, 1 - par, 1, True)
                    if v == 6 and not last:
                        copy_at(b + 1, False)
                    if v == 9 and first:
                        scale_at(0, 0)
                    if v == 21 and not last:
                        scale_at(b + 1, 1 - par)
                    if v == 11 and not first:
                        copy_hmt(b - 1, isinstance(b, int) and b == 1)
                    if v == 14:
                        copy_sums(b, par, 0, isinstance(b, int) and b < 2)
                    if v == 17 and not last:
                        copy_p(b + 1, 1 - par, first)
                    if v == 18 and not last:
                        copy_q(1 - par)
                    if v == 19 and par == 0 and not last_pair:
                        copy_xt(b // 2 + 1)
                    if v == 23 and par == 0 and not first:
                        copy_x1t(b // 2 - 1)

            graphs(act, graph)
            copy_sums(NB - 1, 1, 1, True)
            copy_hmt(NB - 1, False)
            copy_x1t(PAIRS - 1)

            def copy_xe(g):
                act.wait_ge(xw_psum, g + 1)
                nc.scalar.activation(xe[g].rearrange("p b f -> p (b f)"), x_bank[g % 4][:, :], ACT.Copy)\
                    .then_inc(xe_ready, 1)

            def normalise(g):
                act.wait_ge(g_ready, g + 1)
                last = g == GROUPS - 1
                for k in range(0, GB, 2 if last else 1):
                    y = x_all[:, GB * g + k]
                    ins = nc.scalar.activation(y, y, ACT.Identity, bias=g_shift[g % 2][:, k:k + 1],
                                               scale=g_scale[g % 2][:, k:k + 1])
                ins.then_inc(yf_ready, 1)

            AHEAD = 5
            for g in range(AHEAD):
                copy_xe(g)
            for g in range(GROUPS):
                if g + AHEAD < GROUPS:
                    copy_xe(g + AHEAD)
                normalise(g)

        @block.vector
        def _(dve):
            steps = [0]

            def link(ins):
                steps[0] += 1
                ins.then_inc(dve_step, 1)
                dve.wait_ge(dve_step, steps[0])

            nc.vector.memset(ones[:, :], 1.0)
            nc.vector.memset(ones_bf[:, :], 1.0)
            for i in range(2):
                nc.vector.memset(w_nat[i][:, :, :], 0.0)
                nc.vector.memset(w_t[i][:, :, :, :], 0.0)
            link(nc.vector.memset(w_bn[:, :, :], 0.0))
            dve.wait_ge(ident_ready, 1)
            nc.vector.tensor_scalar(neg_big[:, :], ident[:, :], -BIG, None, ALU.mult)
            dve.wait_ge(w1_in, 32)
            nc.vector.tensor_tensor(w_sign[:, 0], w_raw[:, 0], w_raw[:, 1], ALU.add)
            link(nc.vector.tensor_scalar(w_sign[:, 1], w_raw[:, 1], -1.0, None, ALU.mult))
            dve.wait_ge(b_in, 32)
            nc.vector.tensor_copy(w_diff[:, :, :], w_sign[:, :, :])
            link(nc.vector.tensor_copy(b1_diff[:, :], b1_row[:, :]))

            def even_units(ap, a, b):
                return ap.rearrange("p (v k h) -> p v k h", k=2, h=HU)[:, a:b, 0]

            for dst, src in ((w_diff[:, 0], w_sign[:, 0]), (w_diff[:, 1], w_sign[:, 1]),
                             (b1_diff[:, :], b1_row[:, :])):
                ins = nc.vector.tensor_tensor(even_units(dst, BANKS // 2, EU), even_units(src, BANKS // 2, EU),
                                              even_units(src, 0, EU - BANKS // 2), ALU.subtract)
            link(ins)

            def reorder(dst, src):
                for q in range(HQ):
                    ins = nc.vector.tensor_copy(
                        dst[:, q].rearrange("p (m c) -> p c m", c=C1),
                        src.rearrange("p (c q m) -> p c q m", c=C1, q=HQ)[:, :, q])
                return ins

            def weights(i):
                rows = slice(F * i, F * i + F)
                for t in range(2):
                    ins = reorder(w_t[i][rows, t], w_diff[rows, t])
                ins.then_inc(w_t_ready, 1)
                nc.vector.tensor_copy(w_nat[i][rows, 0], w_sign[rows, 0])
                nc.vector.tensor_copy(w_nat[i][rows, 1], w_raw[rows, 1]).then_inc(weights_ready, 1)

            def fill_wq(i, c):
                dve.wait_ge(pats_ready, 1)
                nc.vector.tensor_copy(wq[i][:, c].rearrange("p s q k -> p s (q k)"),
                                      pat_w[:, :].unsqueeze(2).broadcast_to([128, SETS, HQ * N]))\
                    .then_inc(wq_init[i], 1)

            reorder(b1_t[:, :, :], b1_diff[:, :])
            weights(0)
            dve.wait_ge(bias_t_psum, 1)
            nc.vector.tensor_copy(b1t_all[:, :], s_bank[1][0:HH, 0:HQ]).then_inc(bias_t_ready, 1)
            fill_wq(0, 0)
            dve.wait_ge(bias_psum, 1)
            nc.vector.tensor_copy(b1_all[:, :], s_bank[0][:, 0:H])
            link(nc.vector.tensor_copy(b2_parts[:, 0], s_bank[0][:, H:H + F]))
            link(nc.vector.tensor_tensor(b2_parts[:, 1], b2_parts[:, 0], hi(b2_parts[:, 0])[:, 1::2], ALU.subtract))
            nc.vector.tensor_tensor(b2_parts[:, 2], b2_parts[:, 1], hi(b2_parts[:, 1])[:, 1::2], ALU.subtract)\
                .then_inc(bias_ready, 1)

            def degree(n, par):
                dve.wait_ge(a_loaded[par], 16 * (n // 2 + 1))
                nc.vector.tensor_reduce(d_now[par][:, :], a_in[par][:, :], AX.X, ALU.add).then_inc(d_done, 1)

            def make_masks(n, par):
                dve.wait_ge(at_copied, n + 1)
                at = at_raw[:, :]
                nc.vector.tensor_scalar(mask[par][:, :], at, 0.0, None, ALU.is_gt).then_inc(masks_made, 1)

            def negative_root(n, par):
                dve.wait_ge(rs_ready, n + 1)
                nc.vector.scalar_tensor_tensor(out=nsd_all[:, bass.ds(n, 1)], in0=d_now[par][:, :], scalar=-1.0,
                                               in1=rs_now[par][:, :], op0=ALU.mult, op1=ALU.mult)\
                    .then_inc(nsd_made, 1)

            def norm_step(o, par, k):
                xo = x_all[:, bass.ds(o, 1)].rearrange("p a f -> p (a f)")
                if k == 0:
                    dve.wait_ge(l0_psum, o + 1)
                    if isinstance(o, int) and o == 0:
                        dve.wait_ge(x_all_in, 16)
                    if par == 0 and not (isinstance(o, int) and o == 0):
                        dve.wait_ge(x1_kept, o // 2)
                        dve.wait_ge(x1t_psum, o // 2)
                    nc.vector.tensor_tensor(x1[:, par], xo, bx[:, 0:F], ALU.add).then_inc(l0_added, 1)
                elif k == 1:
                    dve.wait_ge(l0_added, o + 1)
                    nc.vector.bn_stats(ln_stats[:, :], x1[:, par]).then_inc(ln_step, 1)
                elif k == 2:
                    nc.vector.bn_aggr(ln_mv[:, :], ln_stats[:, :]).then_inc(var_ready, 1)

            degree(0, 0)
            make_masks(0, 0)
            weights(1)
            negative_root(0, 0)
            for c in range(C1 - 1):
                fill_wq(1, c)

            def graph(b, par, first, last, last_pair=False):
                for w in range(EU):
                    if w == 16 and not first:
                        if not (isinstance(b, int) and b == 1):
                            dve.wait_ge(x1_ready, b - 1)
                        dve.wait_ge(ln_step, b)
                    dve.wait_ge(d_for_dve, EU * b + w + 1)
                    if not (first and w < RING):
                        dve.wait_ge(contracted, UNITS * b + 2 * (w - RING) + 2)
                    nc.vector.scalar_tensor_tensor(
                        out=ind_v[w % RING][:, :].rearrange("p (h k) -> p h k", k=N),
                        in0=d_bank[(2 * w + 1) % BANKS][:, :].rearrange("p (h k) -> p h k", k=N), scalar=0.0,
                        in1=mask[par][:, :].unsqueeze(1).broadcast_to([128, HU, N]),
                        op0=ALU.is_gt, op1=ALU.mult).then_inc(dve_ind, 1)
                    if w == 0 and not last:
                        degree(b + 1, 1 - par)
                    if w in (14, 15, 16) and not first:
                        norm_step(b - 1, 1 - par, w - 14)
                    if w == 17 and not last:
                        make_masks(b + 1, 1 - par)
                    if w == 11 and not last:
                        negative_root(b + 1, 1 - par)
                    if last_pair and w % 6 == 5 and (w // 6 < 3 or last):
                        chunk_stats(4 * par + w // 6 - par)

            def chunk_stats(i):
                w = PAIRS * N // 8
                dve.wait_ge(x1t_copied, (i + 1) * PAIRS // 8)
                nc.vector.bn_stats(bn_st[:, i], x1t_all[:, :, :].rearrange("p a k -> p (a k)")[:, w * i:w * i + w])\
                    .then_inc(stats_made, 1)

            graphs(dve, graph)
            nc.vector.memset(havg[:, :], 0.0)
            link(nc.vector.memset(hdif[:, :], 0.0))
            for i in range(2):
                for j in range(2):
                    r, c = slice(F * i, F * i + F), slice(F * j, F * j + F)
                    src = ident[r, r]
                    nc.vector.tensor_scalar(havg[r, c], src, 0.5, None, ALU.mult)
                    ins = nc.vector.tensor_scalar(hdif[r, c], src, -0.5 if i else 0.5, None, ALU.mult)
            link(ins)
            dve.wait_ge(s_copied, 2 * NB)
            dve.wait_ge(hmt_psum, NB - 1)
            dve.wait_ge(hm_ready, NB - 1)
            link(nc.vector.tensor_tensor(hm[:, :, :], pn[1][:, :].rearrange("p (t h) -> p t h", t=2),
                                         sums[1][:, :, PARTS], ALU.mult))
            for i in range(PARTS):
                ins = nc.vector.tensor_tensor(hm[:, :, :], hm[:, :, :], sums[1][:, :, i], ALU.subtract)
                if i < PARTS - 1:
                    link(ins)
            ins.then_inc(hm_ready, 1)
            for k in range(3):
                if k == 2:
                    dve.wait_ge(x1_ready, NB - 1)
                    dve.wait_ge(ln_step, NB)
                norm_step(NB - 1, 1, k)

            chunk_stats(7)
            dve.wait_ge(stats_made, 8)
            nc.vector.bn_aggr(bn_mv[:, :], bn_st[:, :, :].rearrange("p a b -> p (a b)")).then_inc(bn_ready, 1)
            dve.wait_ge(bn_comb, 1)
            link(nc.vector.tensor_copy(bn[:, 0:3], bx[:, 0:3]))
            link(nc.vector.tensor_tensor(bn[:, 3:4], bn[:, 2:3], bn[:, 2:3], ALU.mult))
            nc.vector.tensor_scalar(bn[:, 3:4], bn[:, 3:4], bn[:, 1:2], EPS, ALU.add, ALU.add).then_inc(bn_var, 1)
            dve.wait_ge(bn_rstd, 1)
            dve.wait_ge(l1_in, 112)
            link(nc.vector.tensor_tensor(bn[:, 5:6], bn[:, 4:5], gb[:, 0:1], ALU.mult))
            for i in range(2):
                r = slice(F * i, F * i + F)
                ins = nc.vector.tensor_scalar(w_bn[r, i], lw[r], bn[r, 5:6], None, ALU.mult)
            ins.then_inc(wbn_ready, 1)
            link(nc.vector.tensor_tensor(bn[:, 6:7], bn[:, 0:1], bn[:, 5:6], ALU.mult))
            link(nc.vector.tensor_tensor(bn[:, 7:8], gb[:, 1:2], bn[:, 6:7], ALU.subtract))
            nc.vector.tensor_copy(shift[:, :], bn[0:F, 7:8].broadcast_to([F, PARTS])).then_inc(shift_ready, 1)
            dve.wait_ge(e_psum, 1)
            link(nc.vector.tensor_copy(e_parts[:, 0], by[0:PARTS, 0:F]))
            for i in range(1, PARTS):
                link(nc.vector.tensor_tensor(e_parts[:, i], e_parts[:, i - 1], hi(e_parts[:, i - 1])[:, 1::2],
                                             ALU.subtract))
            link(nc.vector.tensor_scalar(e_sel[:, :], e_parts[:, 0], ident[0:PARTS, 0:1], None, ALU.mult))
            for i in range(1, PARTS):
                ins = nc.vector.scalar_tensor_tensor(out=e_sel[:, :], in0=e_parts[:, i], scalar=ident[0:PARTS, i:i + 1],
                                                     in1=e_sel[:, :], op0=ALU.mult, op1=ALU.add)
                if i < PARTS - 1:
                    link(ins)
            ins.then_inc(e_ready, 1)

            def grouped(bank):
                return bank[:, :].rearrange("p (b f) -> p b f", f=F)

            def scale_ax(g):
                dve.wait_ge(ax_psum, g + 1)
                if g == 0:
                    dve.wait_ge(nsd_made, NB)
                nc.vector.tensor_tensor(zz[g], grouped(a_bank[g % 4]),
                                        nsd_all[:, GB * g:GB * g + GB].unsqueeze(2).broadcast_to([128, GB, F]),
                                        ALU.mult).then_inc(zz_ready, 1)

            def leaky(g):
                dve.wait_ge(zz_ready, g + 1)
                nc.vector.scalar_tensor_tensor(out=zz[g], in0=zz[g], scalar=0.01, in1=zz[g],
                                               op0=ALU.mult, op1=ALU.max).then_inc(zl_ready, 1)

            def stats(g):
                i = g % 2
                dve.wait_ge(y2_ready, g + 1)
                for k in range(GB):
                    ins = nc.vector.bn_stats(g_st[i][:, k], x_all[:, GB * g + k])
                link(ins)
                if g >= 2:
                    dve.wait_ge(g_ready, g - 1)
                for k in range(GB):
                    ins = nc.vector.bn_aggr(g_mv[i][:, k], g_st[i][:, k])
                link(ins)
                nc.vector.tensor_scalar(g_mv[i][:, :, 0], g_mv[i][:, :, 0], -1.0, None, ALU.mult)
                nc.vector.tensor_scalar(g_mv[i][:, :, 1], g_mv[i][:, :, 1], EPS, None, ALU.add).then_inc(g_mv_ready, 1)

            for g in range(GROUPS + 1):
                if g < GROUPS:
                    scale_ax(g)
                    leaky(g)
                if g >= 1:
                    stats(g - 1)
            dve.wait_ge(g_ready, GROUPS)
            i = (GROUPS - 1) % 2
            for k in range(1, GB, 2):
                y = x_all[:, GB * (GROUPS - 1) + k]
                ins = nc.vector.tensor_scalar(y, y, g_scale[i][:, k:k + 1], g_shift[i][:, k:k + 1],
                                              ALU.mult, ALU.add)
            ins.then_inc(last_ready, 1)

        @block.tensor
        def _(pe):
            def transpose_xt(pair):
                pe.wait_ge(x_loaded, 16 * (pair + 1))
                nc.tensor.transpose(by[:, 0:N], x_in[:, :, :].rearrange("p b f -> p (b f)"), ident[:, :])\
                    .then_inc(xt_psum, 1)

            def transpose_at(n, par):
                pe.wait_ge(a_loaded[par], 16 * (n // 2 + 1))
                nc.tensor.transpose(by[:, 0:N], a_in[par][:, :], ident[:, :]).then_inc(at_psum, 1)

            def project_t(n, par):
                for t in range(2):
                    for q in range(HQ):
                        k = (HQ * t + q) * N
                        ins = nc.tensor.matmul(bx[0:HH, k:k + N], w_t[par][:, t, q], xt[:, :], start=True, stop=True)
                ins.then_inc(t_psum, 1)

            def project_pq(n, par):
                nc.tensor.matmul(bx[:, 0:2 * H], xt[:, :], w_nat[par][:, :, :].rearrange("p t h -> p (t h)"),
                                 start=True, stop=True).then_inc(pq_psum, 1)

            def transpose_hm(o):
                pe.wait_ge(hm_ready, o + 1)
                for t in range(2):
                    ins = nc.tensor.transpose(by[0:HH, N * t:N * t + N], hm[:, t], ident[:, :])
                ins.then_inc(hmt_psum, 1)

            def layer0(o, par):
                pe.wait_ge(hmt_copied, o + 1)
                for t in range(2):
                    nc.tensor.matmul(bx[:, 0:F], hm_t[:, t], w2_sb[:, t], start=(t == 0), stop=False)
                for i in range(PARTS):
                    ins = nc.tensor.matmul(bx[:, 0:F], mask[par][:, :], hi(b2_parts[:, i])[:, 1::2],
                                           start=False, stop=(i == PARTS - 1))
                ins.then_inc(l0_psum, 1)

            def transpose_x1(pair):
                pe.wait_ge(x1_ready, 2 * pair + 2)
                nc.tensor.transpose(by[:, 0:N], x1[:, :, :].rearrange("p b f -> p (b f)"), ident[:, :])\
                    .then_inc(x1t_psum, 1)

            def contract(u, par):
                ring = ind_v if u % 2 else ind_a
                half, col = divmod(HU * u, HH)
                sums_out = s_bank[half][:, 0:(PARTS + 1) * HH].rearrange("p (i h) -> p i h", i=PARTS + 1)
                qv = hi(qn[par][:, :, :].rearrange("p i h -> p (i h)")).rearrange(
                    "p (i h e) -> p i h e", i=PARTS + 1, e=2)
                for h in range(HU):
                    ins = nc.tensor.matmul(sums_out[:, :, col + h],
                                           ring[(u // 2) % RING][:, N * h:N * h + N],
                                           qv[:, :, HU * u + h, 1], start=True, stop=True)
                ins.then_inc(contracted, 1)

            def difference(u, par):
                c, s = divmod(u, SETS)
                c1, q = divmod(c, HQ)
                bank = d_bank[u % BANKS]
                if u in (0, 2):
                    nc.tensor.matmul(bank[:, :].rearrange("p (h k) -> p h k", k=N), neg_big[:, :],
                                     nmask[par][:, :].unsqueeze(1).broadcast_to([128, HU, N]),
                                     start=True, stop=True, skip_group_check=True)
                wv = hi(wq[par][:, c1, s, q])[:, 1::2]
                m = hi(mv[par][:, :, :, :, :].rearrange("p h c q k -> p (h c q k)")).rearrange(
                    "p (h c q k e) -> p h c q k e", h=HU, c=C1, q=HQ, e=2)[:, :, c1, q, :, 1]
                nc.tensor.matmul(bank[:, :].rearrange("p (h k) -> p h k", k=N), wv, m, start=bool(u % 2), stop=True,
                                 skip_group_check=True)\
                    .then_inc(d_for_dve if u % 2 else d_for_act, 1)

            pe.wait_ge(ident_ready, 1)
            transpose_xt(0)
            pe.wait_ge(xt_copied, 1)
            transpose_at(0, 0)
            pe.wait_ge(w_t_ready, 1)
            for q in range(HQ):
                ins = nc.tensor.matmul(s_bank[1][0:HH, q:q + 1], b1_t[:, q], ones[:, 0:1], start=True, stop=True)
            ins.then_inc(bias_t_psum, 1)
            project_t(0, 0)
            nc.tensor.matmul(s_bank[0][:, 0:H], ones[:, :], b1_row[:, :], start=True, stop=True)
            nc.tensor.matmul(s_bank[0][:, H:H + F], ones[:, :], b2_row[:, :], start=True, stop=True)\
                .then_inc(bias_psum, 1)
            pe.wait_ge(t_copied, 2)
            pe.wait_ge(weights_ready, 1)
            project_pq(0, 0)
            pe.wait_ge(qn_ones, 2)
            pe.wait_ge(w2_in, 16)
            pe.wait_ge(weights_ready, 2)
            pe.wait_ge(bias_ready, 1)

            def graph(b, par, first, last, last_pair=False):
                for u in range(UNITS):
                    if u == 0 and not last:
                        pe.wait_ge(pq_copied, b + 1)
                        if par == 1:
                            pe.wait_ge(xt_copied, b // 2 + 2)
                        project_t(b + 1, 1 - par)
                    if u == 6 and not last:
                        if par == 1:
                            pe.wait_ge(xt_copied, b // 2 + 2)
                            if not (isinstance(b, int) and b == 1):
                                pe.wait_ge(x1t_copied, b // 2)
                        elif first:
                            pe.wait_ge(at_copied, 1)
                        else:
                            pe.wait_ge(hmt_copied, b - 1)
                        transpose_at(b + 1, 1 - par)
                    if u == 22 and not first:
                        if last:
                            pe.wait_ge(x1t_copied, b // 2)
                        else:
                            pe.wait_ge(at_copied, b + 2)
                        transpose_hm(b - 1)
                    if u == 28 and not first:
                        if last:
                            pe.wait_ge(pq_copied, b + 1)
                        else:
                            pe.wait_ge(t_copied, 2 * b + 4)
                        layer0(b - 1, 1 - par)
                    if u == 34 and not last:
                        if first:
                            pe.wait_ge(t_copied, 2 * b + 4)
                        else:
                            pe.wait_ge(l0_added, b)
                        project_pq(b + 1, 1 - par)
                    if u == 38 and par == 0 and not last_pair:
                        if first:
                            pe.wait_ge(at_copied, b + 2)
                        else:
                            pe.wait_ge(hmt_copied, b)
                        transpose_xt(b // 2 + 1)
                    if u == 45 and par == 0 and not first:
                        if last_pair:
                            pe.wait_ge(hmt_copied, b)
                        else:
                            pe.wait_ge(xt_copied, b // 2 + 2)
                        transpose_x1(b // 2 - 1)
                    if u == 0:
                        pe.wait_ge(wq_loaded, 16 * WLOADS * (b + 1))
                        pe.wait_ge(mv_loaded, 16 * (b + 1))
                        pe.wait_ge(nmask_made, b + 1)
                    if not (first and u < BANKS):
                        pe.wait_ge(dve_ind if u % 2 else act_ind, EU * b + u // 2 - 1)
                    difference(u, par)
                    if u == LAG:
                        pe.wait_ge(q_split, b + 1)
                        if not first:
                            pe.wait_ge(s_copied, 2 * b - 1)
                    if u == LAG + HALF_UNITS and not first:
                        pe.wait_ge(s_copied, 2 * b)
                    if u >= LAG:
                        contract(u - LAG, par)
                    elif not first:
                        contract(UNITS + u - LAG, 1 - par)

            graphs(pe, graph)
            pe.wait_ge(act_ind, EU * NB)
            pe.wait_ge(dve_ind, EU * NB)
            for u in range(UNITS - LAG, UNITS):
                contract(u, 1)
            pe.wait_ge(hmt_copied, NB - 1)
            transpose_hm(NB - 1)
            pe.wait_ge(l0_added, NB - 1)
            layer0(NB - 1, 1)
            transpose_x1(PAIRS - 1)

            pe.wait_ge(bn_ready, 1)
            nc.tensor.matmul(bx[:, 0:2], havg[:, :], bn_mv[:, :], start=True, stop=True)
            nc.tensor.matmul(bx[:, 2:3], hdif[:, :], bn_mv[:, 0:1], start=True, stop=True).then_inc(bn_comb, 1)

            def project_x(g):
                if g >= 4:
                    pe.wait_ge(xe_ready, g - 3)
                for k in range(GB // 2):
                    nc.tensor.matmul(x_bank[g % 4][:, 2 * F * k:2 * F * k + 2 * F],
                                     x1t_all[:, GB // 2 * g + k], w_bn[:, :, :].rearrange("p a f -> p (a f)"),
                                     start=(k == 0), stop=False, skip_group_check=True)

            def add_e(g):
                nc.tensor.matmul(x_bank[g % 4][:, :].rearrange("p (b f) -> p b f", f=F), ones_bf[:, :],
                                 hi(e_sel[:, :])[:, 1::2].unsqueeze(1).broadcast_to([PARTS, GB, F]),
                                 start=False, stop=True, skip_group_check=True).then_inc(xw_psum, 1)

            pe.wait_ge(wbn_ready, 1)
            project_x(0)
            pe.wait_ge(shift_ready, 1)
            nc.tensor.matmul(by[0:PARTS, 0:F], shift[:, :], lw[0:F], start=True, stop=False)
            nc.tensor.matmul(by[0:PARTS, 0:F], ones[:, 0:PARTS], lb_row[:, :], start=False, stop=True)\
                .then_inc(e_psum, 1)
            for g in range(1, 4):
                project_x(g)
            pe.wait_ge(e_ready, 1)
            for g in range(4):
                add_e(g)
            pe.wait_ge(at_scaled, NB)
            for g in range(GROUPS):
                pe.wait_ge(xe_ready, g + 1)
                if g >= 4:
                    pe.wait_ge(zz_ready, g - 3)
                for k in range(GB):
                    ins = nc.tensor.matmul(a_bank[g % 4][:, F * k:F * k + F], at_all[:, GB * g + k],
                                           xe[g][:, k], start=True, stop=True)
                ins.then_inc(ax_psum, 1)
                if g + 4 < GROUPS:
                    project_x(g + 4)
                    add_e(g + 4)


_INS = ["x", "adj", "L0_gnn_W1", "L0_gnn_b1", "L0_gnn_W2", "L0_gnn_b2",
        "L1_gnn_gamma", "L1_gnn_beta", "L1_gnn_W", "L1_gnn_b"]
_OUTS = [((64, 128, 64), "float32")]


def kernel(**inputs):
    import numpy as _np
    import concourse.bacc as _bacc
    from concourse import mybir as _mybir
    from concourse.bass_utils import run_bass_kernel_spmd as _run

    nc = _bacc.Bacc("TRN2", target_bir_lowering=False, num_devices=1)
    arrays, args = {}, []
    for name in _INS:
        a = _np.ascontiguousarray(inputs[name])
        arrays[f"in_{name}_dram"] = a
        args.append(nc.dram_tensor(f"in_{name}_dram", a.shape, _mybir.dt.from_np(a.dtype), kind="ExternalInput").ap())
    for i, (shape, dtype) in enumerate(_OUTS):
        dt = _mybir.dt.from_np(_np.dtype(dtype))
        args.append(nc.dram_tensor(f"out_{i}_dram", shape, dt, kind="ExternalOutput").ap())
    gnn_kernel(nc, *args)
    r = _run(nc, [arrays], core_ids=[0])
    return r.results[0]["out_0_dram"]
```
